# Optimizing a Trainium2 kernel written in Bass

```python
import numpy as np
import jax
import jax.numpy as jnp

def _softmax(x, axis=-1):
    return jax.nn.softmax(x, axis=axis)

def _gelu(x):
    return jax.nn.gelu(x, approximate=True)

def _silu(x):
    return jax.nn.silu(x)

def _sigmoid(x):
    return jax.nn.sigmoid(x)

def _layernorm(x, axis=-1, eps=1e-05):
    m = jnp.mean(x, axis=axis, keepdims=True)
    v = jnp.var(x, axis=axis, keepdims=True)
    return (x - m) / jnp.sqrt(v + eps)

def _scatter_add(tgt, idx, src, axis=0):
    return tgt.at[idx].add(src)

def _segment_sum(src, seg, n):
    return jax.ops.segment_sum(src, seg, n)
kernel_name = 'mk_gnn_resnorm_d1_gnn_r8_aac23d'

def setup_inputs(seed: int=0):
    np.random.seed(seed)
    _w = jnp.asarray

    def _rec_inputs():
        import jax
        import jax.numpy as jnp
        _gk = jax.random.key(seed)
        x = -0.0005121 + 1.001 * jax.random.normal(jax.random.fold_in(_gk, 1), (6250, 64), jnp.float32)
        src = jax.random.randint(jax.random.fold_in(_gk, 2), (200000,), 0, 6250, jnp.int32)
        dst = jax.random.randint(jax.random.fold_in(_gk, 3), (200000,), 0, 6250, jnp.int32)
        _o = jnp.argsort(dst, stable=True)
        src = src[_o]
        dst = dst[_o]
        edge_attr_64 = 0.000135552 + 1.00015 * jax.random.normal(jax.random.fold_in(_gk, 11), (200000, 64), jnp.float32)
        edge_weight = jax.random.uniform(jax.random.fold_in(_gk, 13), (200000,), jnp.float32, 0.0, 0.999998)
        return (x, src, dst, edge_attr_64, edge_weight)
    x, src, dst, edge_attr_64, edge_weight = _rec_inputs()

    def _L0_gnn_setup():
        import jax, jax.numpy as jnp
        import numpy as np
        N = 6250
        E = 100000
        DIN = 64
        DOUT = 64
        K = 5

        def _mixed(x, weights, edge_weights, edge_attr, Wgcn, bgcn, Wsage_s, Wsage_n, bsage, gin_eps, Wgin, bgin, Wgc1, Wgc2, bgc, Wedge, bedge, src, dst):
            n = x.shape[0]
            seg = lambda v: jax.ops.segment_sum(v, dst, num_segments=n)
            xs = x[src]
            deg_w = jnp.maximum(seg(edge_weights), 1.0)
            deg_c = jnp.maximum(seg(jnp.ones_like(edge_weights)), 1.0)
            norm = edge_weights / jnp.sqrt(deg_w[src] * deg_w[dst])
            gcn = seg(norm[:, None] * xs) @ Wgcn + bgcn
            sage = x @ Wsage_s + seg(xs) / deg_c[:, None] @ Wsage_n + bsage
            agg_w = seg(edge_weights[:, None] * xs)
            gin = ((1.0 + gin_eps) * x + agg_w) @ Wgin + bgin
            gconv = x @ Wgc1 + agg_w @ Wgc2 + bgc
            eop = seg(edge_weights[:, None] * jax.nn.relu(xs + edge_attr)) @ Wedge + bedge
            ops = jnp.stack([gcn, sage, gin, gconv, eop])
            return jnp.einsum('k,knd->nd', weights, ops)
        key = jax.random.key(seed)
        ks = jax.random.split(key, 18)
        s = 1.0 / np.sqrt(DIN)
        f32 = jnp.float32
        return {'x': jax.random.normal(ks[0], (N, DIN), f32), 'weights': jax.random.uniform(ks[1], (K,), f32), 'edge_weights': jax.random.uniform(ks[2], (E,), f32), 'edge_attr': jax.random.normal(ks[3], (E, DIN), f32), 'Wgcn': jax.random.normal(ks[4], (DIN, DOUT), f32) * s, 'bgcn': jnp.zeros((DOUT,), f32), 'Wsage_s': jax.random.normal(ks[5], (DIN, DOUT), f32) * s, 'Wsage_n': jax.random.normal(ks[6], (DIN, DOUT), f32) * s, 'bsage': jnp.zeros((DOUT,), f32), 'gin_eps': jnp.zeros((), f32), 'Wgin': jax.random.normal(ks[7], (DIN, DOUT), f32) * s, 'bgin': jnp.zeros((DOUT,), f32), 'Wgc1': jax.random.normal(ks[8], (DIN, DOUT), f32) * s, 'Wgc2': jax.random.normal(ks[9], (DIN, DOUT), f32) * s, 'bgc': jnp.zeros((DOUT,), f32), 'Wedge': jax.random.normal(ks[10], (DIN, DOUT), f32) * s, 'bedge': jnp.zeros((DOUT,), f32), 'edge_index': jax.random.randint(ks[11], (2, E), 0, N), 'with_linear': 0}
    _L0_gnn_all = _L0_gnn_setup()
    _L0_gnn_in = {k: v for k, v in _L0_gnn_all.items() if k in ('weights', 'Wgcn', 'bgcn', 'Wsage_s', 'Wsage_n', 'bsage', 'gin_eps', 'Wgin', 'bgin', 'Wgc1', 'Wgc2', 'bgc', 'Wedge', 'bedge')}
    del _L0_gnn_all
    return {'x': x, 'src': src, 'dst': dst, 'edge_attr_64': edge_attr_64, 'edge_weight': edge_weight, 'L0_gnn_weights': _L0_gnn_in['weights'], 'L0_gnn_Wgcn': _L0_gnn_in['Wgcn'], 'L0_gnn_bgcn': _L0_gnn_in['bgcn'], 'L0_gnn_Wsage_s': _L0_gnn_in['Wsage_s'], 'L0_gnn_Wsage_n': _L0_gnn_in['Wsage_n'], 'L0_gnn_bsage': _L0_gnn_in['bsage'], 'L0_gnn_gin_eps': _L0_gnn_in['gin_eps'], 'L0_gnn_Wgin': _L0_gnn_in['Wgin'], 'L0_gnn_bgin': _L0_gnn_in['bgin'], 'L0_gnn_Wgc1': _L0_gnn_in['Wgc1'], 'L0_gnn_Wgc2': _L0_gnn_in['Wgc2'], 'L0_gnn_bgc': _L0_gnn_in['bgc'], 'L0_gnn_Wedge': _L0_gnn_in['Wedge'], 'L0_gnn_bedge': _L0_gnn_in['bedge']}

def reference(x, src, dst, edge_attr_64, edge_weight, L0_gnn_weights, L0_gnn_Wgcn, L0_gnn_bgcn, L0_gnn_Wsage_s, L0_gnn_Wsage_n, L0_gnn_bsage, L0_gnn_gin_eps, L0_gnn_Wgin, L0_gnn_bgin, L0_gnn_Wgc1, L0_gnn_Wgc2, L0_gnn_bgc, L0_gnn_Wedge, L0_gnn_bedge):
    import jax
    import jax.numpy as jnp

    def _L0_gnn_ref(x, weights, edge_weights, edge_attr, Wgcn, bgcn, Wsage_s, Wsage_n, bsage, gin_eps, Wgin, bgin, Wgc1, Wgc2, bgc, Wedge, bedge, edge_index, with_linear):
        import jax, jax.numpy as jnp
        import numpy as np
        N = 6250
        E = 100000
        DIN = 64
        DOUT = 64
        K = 5

        def _mixed(x, weights, edge_weights, edge_attr, Wgcn, bgcn, Wsage_s, Wsage_n, bsage, gin_eps, Wgin, bgin, Wgc1, Wgc2, bgc, Wedge, bedge, src, dst):
            n = x.shape[0]
            seg = lambda v: jax.ops.segment_sum(v, dst, num_segments=n)
            xs = x[src]
            deg_w = jnp.maximum(seg(edge_weights), 1.0)
            deg_c = jnp.maximum(seg(jnp.ones_like(edge_weights)), 1.0)
            norm = edge_weights / jnp.sqrt(deg_w[src] * deg_w[dst])
            gcn = seg(norm[:, None] * xs) @ Wgcn + bgcn
            sage = x @ Wsage_s + seg(xs) / deg_c[:, None] @ Wsage_n + bsage
            agg_w = seg(edge_weights[:, None] * xs)
            gin = ((1.0 + gin_eps) * x + agg_w) @ Wgin + bgin
            gconv = x @ Wgc1 + agg_w @ Wgc2 + bgc
            eop = seg(edge_weights[:, None] * jax.nn.relu(xs + edge_attr)) @ Wedge + bedge
            ops = jnp.stack([gcn, sage, gin, gconv, eop])
            return jnp.einsum('k,knd->nd', weights, ops)
        src, dst = (edge_index[0], edge_index[1])
        return _mixed(x, weights, edge_weights, edge_attr, Wgcn, bgcn, Wsage_s, Wsage_n, bsage, gin_eps, Wgin, bgin, Wgc1, Wgc2, bgc, Wedge, bedge, src, dst)
    edge_index = jnp.stack([src, dst])
    x = _layernorm(x + _L0_gnn_ref(x, L0_gnn_weights, edge_weight, edge_attr_64, L0_gnn_Wgcn, L0_gnn_bgcn, L0_gnn_Wsage_s, L0_gnn_Wsage_n, L0_gnn_bsage, L0_gnn_gin_eps, L0_gnn_Wgin, L0_gnn_bgin, L0_gnn_Wgc1, L0_gnn_Wgc2, L0_gnn_bgc, L0_gnn_Wedge, L0_gnn_bedge, edge_index, 0), axis=-1)
    return x

_drawn_inputs = setup_inputs


def setup_inputs(seed=0):
    import zlib

    import numpy as np

    out = dict(_drawn_inputs(seed))
    spreads = {'L0_gnn_bgcn': (0.0, 2.0),
     'L0_gnn_bsage': (0.0, 2.0),
     'L0_gnn_bgin': (0.0, 0.396),
     'L0_gnn_bgc': (0.0, 0.627),
     'L0_gnn_bedge': (0.0, 0.8)}
    factors = {'L0_gnn_Wgcn': 64.0, 'L0_gnn_Wsage_s': 8.0, 'L0_gnn_Wsage_n': 45.703}
    for name, (base, spread) in spreads.items():
        noise = np.random.default_rng([zlib.crc32(name.encode()), seed]).standard_normal(out[name].shape)
        drawn = base * np.exp(spread * noise) if base else spread * noise
        out[name] = jnp.asarray(drawn.astype(out[name].dtype))
    for name, factor in factors.items():
        out[name] = (out[name] * factor).astype(out[name].dtype)
    return out
```

```python
from contextlib import ExitStack

import concourse.bass as bass
import numpy as np
from concourse import mybir

F32 = mybir.dt.float32
BF16 = mybir.dt.bfloat16
I32 = mybir.dt.int32
U32 = mybir.dt.uint32
ALU = mybir.AluOpType
ACT = mybir.ActivationFunctionType
AX = mybir.AxisListType

P = 128
N, D = 6250, 64
E = 200000
TILES = 8
CHUNK = P * TILES
CHUNKS = -(-E // CHUNK)
LAST_START = E - CHUNK
LAST_NEW = E - (CHUNKS - 1) * CHUNK
UNROLL = 4
STEPS = CHUNKS // UNROLL
WINDOW = 64
WINDOWS = -(-N // WINDOW)
NT = -(-N // P)
NPAD = P * NT
SUMS = NPAD + WINDOW
TROW = D + 4
BLOCK = 3 * D + TROW
DEG_CHUNKS = 2
FAR = 1.0e6
EPS = 1e-5
GROUP = 7
assert CHUNKS == STEPS * UNROLL and NT % GROUP == 0 and UNROLL == 2 * DEG_CHUNKS


def build(nc, x, src, dst, edge_attr, edge_weight, mix, Wgcn, bgcn, Wsage_s, Wsage_n, bsage,
          gin_eps, Wgin, bgin, Wgc1, Wgc2, bgc, Wedge, bedge, out):
    ctx = ExitStack()
    with ctx:
        def sb(name, shape, dt=F32):
            return ctx.enter_context(nc.sbuf_tensor(name, shape, dt))

        def pb(name, shape):
            return ctx.enter_context(nc.psum_tensor(name, shape, F32))

        def sem(name):
            return ctx.enter_context(nc.semaphore(name))

        table = nc.dram_tensor("node_table", [NPAD, TROW], F32, kind="Internal").ap()

        LOW, HIGH = P, CHUNKS - P
        groups = ((0, P), (1, HIGH))
        area = sb("area", [P, NPAD])
        raw_src, raw_dst = (area[:, k * 2 * CHUNK:(k + 1) * 2 * CHUNK].bitcast(I32).rearrange("p (g e) -> p g e", g=2)
                            for k in range(2))
        row_w = area[:, 4 * CHUNK:6 * CHUNK].rearrange("p (g e) -> p g e", g=2)
        attr = sb("attr", [P, UNROLL, TILES, D])
        feat = sb("feat", [P, UNROLL, TILES, BLOCK])
        attr_flat, feat_flat = (t[:, :, :, :].rearrange("p u j b -> p (u j b)") for t in (attr, feat))
        row_src, row_real = attr_flat[:, 0:CHUNK], attr_flat[:, CHUNK:2 * CHUNK]
        hot = sb("hot", [P, UNROLL, TILES, WINDOW])
        row_dst = hot[:, :, :, :].rearrange("p u j n -> p (u j n)").rearrange("p (g e) -> p g e", g=2)
        least = sb("least", [P, 2])
        most = sb("most", [P, 2])
        unfit = sb("unfit", [P, 2])
        unfit_any = sb("unfit_any", [P, 1])
        fits = sb("fits", [P, 1])
        base = sb("base", [P, 2])
        base_row = sb("base_row", [1, CHUNKS], I32)
        passes = sb("passes", [1, 1], I32)
        e_src = sb("e_src", [P, CHUNKS, TILES], U32)
        e_dst = sb("e_dst", [P, CHUNKS, TILES])
        e_win = sb("e_win", [P, CHUNKS, TILES], BF16)
        e_tmp = sb("e_tmp", [P, CHUNKS, TILES])
        e_w = sb("e_w", [P, CHUNKS, TILES])
        w_parts = sb("w_parts", [P, CHUNKS, TILES, 4], BF16)
        ident = sb("ident", [P, P])
        ones = sb("ones", [P, P])
        iota_b = sb("iota_b", [P, WINDOW], BF16)
        win_off = sb("win_off", [P, 1])
        part_sel = sb("part_sel", [4, 2])
        part_ones = sb("part_ones", [4, 2])
        w_stage = sb("w_stage", [P, 2, DEG_CHUNKS, TILES, 4], BF16)
        hot_b = sb("hot_b", [P, 2, DEG_CHUNKS * TILES, WINDOW], BF16)
        deg_sum = feat_flat[0:4, 0:SUMS]
        deg_max = sb("deg_max", [P, NT, 2])
        deg_root = sb("deg_root", [P, NT])
        inv_root = sb("inv_root", [P, NT])
        inv_count = sb("inv_count", [P, NT])
        table_sb = sb("table_sb", [P, NT, TROW])
        idx = sb("idx", [P, UNROLL, TILES], U32)
        wroot = sb("wroot", [P, UNROLL, TILES])
        sums = sb("sums", [P, 2, SUMS])
        xT = area[0:D + 1, :]
        W_in = sb("W_in", [P, 7, D])
        b_in = sb("b_in", [D + 1, 5, D])
        mix_sb = sb("mix_sb", [P, 5])
        eps_sb = sb("eps_sb", [P, 1])
        eps_ln = sb("eps_ln", [P, 1])
        gin_scale = sb("gin_scale", [P, 1])
        W_node = sb("W_node", [D + 1, D])
        W_low = sb("W_low", [P, 2, D])
        W_high = sb("W_high", [P, 2, D])
        h = feat_flat[:, 0:NT * D].rearrange("p (t d) -> p t d", d=D)
        h_tmp = feat_flat[:, NT * D:(NT + 2 * GROUP) * D].rearrange("p (k t d) -> p k t d", k=2, d=D)
        squares = attr_flat[:, 0:GROUP * D].rearrange("p (t d) -> p t d", d=D)
        mean = sb("mean", [P, NT])
        var = sb("var", [P, NT])

        acc_ps = [pb(f"acc_ps{i}", [P, 512]) for i in range(2)]
        flip_ps = [pb(f"flip_ps{i}", [P, 512]) for i in range(2)]
        misc_ps = pb("misc_ps", [P, 512])
        node_ps, gcn_ps, sage_ps = (pb(n, [P, 512]) for n in ("node_ps", "gcn_ps", "sage_ps"))

        dst_loaded, src_loaded, w_loaded = sem("dst_loaded"), sem("src_loaded"), sem("w_loaded")
        pad_dst, pad_src, pad_w, pad_x = (sem(f"pad_{n}") for n in ("dst", "src", "w", "x"))
        x_loaded, small_loaded = sem("x_loaded"), sem("small_loaded")
        consts = sem("consts")
        gathers_begun, windows_set = sem("gathers_begun"), sem("windows_set")
        dve_chain, pass_step = sem("dve_chain"), sem("pass_step")
        pool_chain = sem("pool_chain")
        unfit_ready, unfit_counted = sem("unfit_ready"), sem("unfit_counted")
        base_ready, base_flipped, base_stored = sem("base_ready"), sem("base_flipped"), sem("base_stored")
        rows_ready, flipped, flip_used = sem("rows_ready"), sem("flipped"), sem("flip_used")
        w_split = sem("w_split")
        w_staged = sem("w_staged")
        hot_b_ready, deg_product, deg_added = sem("hot_b_ready"), sem("deg_product"), sem("deg_added")
        deg_nodes, root_in, root_out = sem("deg_nodes"), sem("root_in"), sem("root_out")
        table_ready, table_stored = sem("table_ready"), sem("table_stored")
        x_flipped, x_flip_used = sem("x_flipped"), sem("x_flip_used")
        staged = sem("staged")
        gathered = [sem(f"gathered{u}") for u in range(UNROLL)]
        attr_loaded = [sem(f"attr_loaded{u}") for u in range(UNROLL)]
        wroot_ready, summed_in = sem("wroot_ready"), sem("summed_in")
        feat_ready = sem("feat_ready")
        chunk_product = sem("chunk_product")
        added = sem("added")
        weights_mixed = sem("weights_mixed")
        out_product, out_taken = sem("out_product"), sem("out_taken")
        centred, squared, var_ready, root_ready = sem("centred"), sem("squared"), sem("var_ready"), sem("root_ready")
        out_ready, stored = sem("out_ready"), sem("stored")

        FLIPS = 3 * 2 * (TILES // 4)
        XFLIPS = -(-NT // 4)
        GROUPS = NT // GROUP

        block = ctx.enter_context(nc.Block())

        def window_at(first, v):
            return nc.s_assert_within(first + v * WINDOW, 0, NPAD,
                                      skip_runtime_bounds_check_because="first is 0 in all passes but the first")

        def rows_of(t, c0, c1):
            return t[c0 * CHUNK:c1 * CHUNK].rearrange("(c e) -> c e", e=CHUNK)

        FULL = CHUNKS - 1 - P
        FULL16 = FULL - FULL % 16

        def load_rows(eng, t, rows, loaded):
            eng.dma_start(rows[:, 0, :], rows_of(t, 0, P)).then_inc(loaded, 16)
            eng.dma_start(rows[0:FULL16, 1, :], rows_of(t, P, P + FULL16)).then_inc(loaded, 16)
            eng.dma_start(rows[FULL16:FULL, 1, :], rows_of(t, P + FULL16, P + FULL)).then_inc(loaded, 16)
            eng.dma_start(rows[FULL:FULL + 1, 1, CHUNK - LAST_NEW:],
                          t[E - LAST_NEW:E].rearrange("(a e) -> a e", a=1)).then_inc(loaded, 16)

        ROWS_LOADED = 4 * 16

        def node_rows(t, rows):
            full = N // NT
            cut = full - full % 16
            v = t[0:full * NT, :].rearrange("(p t) d -> p t d", t=NT)
            rest = N - full * NT
            return ((v[0:cut], rows[0:cut]), (v[cut:full], rows[cut:full]),
                    (t[full * NT:N, :].rearrange("(p t) d -> p t d", p=1), rows[full:full + 1, 0:rest]))

        X_LOADED = 3 * 16

        @block.sync
        def _(sp):
            sp.wait_ge(pad_dst, 1)
            load_rows(sp, dst, raw_dst, dst_loaded)
            sp.wait_ge(pad_src, 1)
            load_rows(sp, src, raw_src, src_loaded)
            sp.wait_ge(pad_x, 1)
            for of, to in node_rows(x, table_sb[:, :, 0:D]):
                sp.dma_start(to, of).then_inc(x_loaded, 16)
            sp.wait_ge(table_ready, 1)
            sp.dma_start(table.rearrange("(p t) d -> p (t d)", p=P),
                         table_sb[:, :, :].rearrange("p t d -> p (t d)")).then_inc(table_stored, 16)
            sp.wait_ge(base_stored, 1)
            n_pass = sp.value_load(passes[0:1, 0:1], min_val=1, max_val=WINDOWS)
            with sp.Fori(0, n_pass) as v:
                with sp.Fori(0, STEPS) as i:
                    for u in range(UNROLL):
                        c = i * UNROLL + u
                        start = c * CHUNK
                        if u == UNROLL - 1:
                            start = nc.s_assert_within(start - (c // (CHUNKS - 1)) * ((CHUNKS - 1) * CHUNK - LAST_START),
                                                       min_val=0, max_val=LAST_START,
                                                       skip_runtime_bounds_check_because="the last chunk is moved back")
                        sp.wait_ge(feat_ready, v * CHUNKS + c + 1)
                        sp.dma_start(attr[:, u, :, :].rearrange("p j d -> p (j d)"),
                                     edge_attr[bass.ds(start, CHUNK), :].rearrange(
                                         "(p j) d -> p (j d)", p=P)).then_inc(attr_loaded[u], 16)
            sp.wait_ge(out_ready, GROUPS)
            for to, of in node_rows(out, h):
                sp.dma_start(to, of).then_inc(stored, 16)
            sp.wait_ge(stored, X_LOADED)

        @block.gpsimd
        def _(pool):
            nc.gpsimd.memset(raw_dst[:, 1, :], int(FAR)).then_inc(pad_dst, 1)
            nc.gpsimd.memset(raw_src[:, 1, :], 0).then_inc(pad_src, 1)
            nc.gpsimd.iota(iota_b[:], [[1, WINDOW]], base=0, channel_multiplier=0,
                           allow_small_or_imprecise_dtypes=True).then_inc(consts, 1)
            nc.gpsimd.memset(ident[:], 0.0).then_inc(pool_chain, 1)
            nc.gpsimd.memset(ones[:], 1.0).then_inc(consts, 1)
            pool.wait_ge(pool_chain, 1)
            nc.gpsimd.affine_select(out=ident[:], in_=ident[:], compare_op=ALU.not_equal, fill=1.0, base=0,
                                    pattern=[[-1, P]], channel_multiplier=1).then_inc(consts, 1)
            nc.gpsimd.memset(part_ones[:], 1.0).then_inc(pool_chain, 1)
            pool.wait_ge(pool_chain, 2)
            nc.gpsimd.affine_select(out=part_sel[:, 0:1], in_=part_ones[:, 0:1], compare_op=ALU.is_ge, fill=0.0,
                                    base=2, pattern=[[0, 1]], channel_multiplier=-1).then_inc(consts, 1)
            nc.gpsimd.affine_select(out=part_sel[:, 1:2], in_=part_ones[:, 1:2], compare_op=ALU.is_ge, fill=0.0,
                                    base=-3, pattern=[[0, 1]], channel_multiplier=1).then_inc(consts, 1)
            pool.wait_ge(table_stored, 16)
            pool.wait_ge(base_stored, 1)
            n_pass = pool.value_load(passes[0:1, 0:1], min_val=1, max_val=WINDOWS)
            with pool.Fori(0, n_pass) as v:
                with pool.Fori(0, STEPS) as i:
                    for u in range(UNROLL):
                        it = v * CHUNKS + i * UNROLL + u
                        pool.wait_ge(staged, it + 1)
                        pool.wait_ge(chunk_product, it + 1)
                        pool.sem_inc(gathers_begun, 1)
                        for j in range(TILES):
                            nc.gpsimd.indirect_dma_start(
                                out=feat[:, u, j, 3 * D:BLOCK], out_offset=None, in_=table,
                                in_offset=bass.IndirectOffsetOnAxis(ap=idx[:, u, j:j + 1], axis=0),
                            ).then_inc(gathered[u], 16)

        @block.scalar
        def _(act):
            act.wait_ge(pad_w, 1)
            load_rows(act, edge_weight, row_w, w_loaded)
            for k, W in enumerate((Wgcn, Wsage_s, Wsage_n, Wgin, Wgc1, Wgc2, Wedge)):
                for half in range(2):
                    act.dma_start(W_in[half * D:(half + 1) * D, k, :], W).then_inc(small_loaded, 16)
            for k, b in enumerate((bgcn, bsage, bgin, bgc, bedge)):
                act.dma_start(b_in[D:D + 1, k, :], b.rearrange("(a d) -> a d", a=1)).then_inc(small_loaded, 16)
            act.dma_start(mix_sb[:, :], mix.rearrange("(a k) -> a k", a=1).to_broadcast([P, 5])).then_inc(small_loaded, 16)
            act.dma_start(eps_sb[:, :], gin_eps.to_broadcast([P, 1])).then_inc(small_loaded, 16)

            act.wait_ge(base_stored, 1)
            n_pass = act.value_load(passes[0:1, 0:1], min_val=1, max_val=WINDOWS)
            act.wait_ge(w_split, 1)
            with act.Fori(0, n_pass) as v:
                with act.Fori(0, STEPS) as i:
                    for s in range(2):
                        step = v * 2 * STEPS + i * 2 + s
                        act.wait_ge(deg_product, step + 1)
                        nc.scalar.copy(w_stage[:, s], w_parts[:, bass.ds(i * UNROLL + s * DEG_CHUNKS, DEG_CHUNKS)]
                                       ).then_inc(w_staged, 1)
            act.wait_ge(root_in, 1)
            nc.scalar.activation(deg_root[:], deg_max[:, :, 0], ACT.Sqrt).then_inc(root_out, 1)
            for q in range(XFLIPS):
                n = min(4, NT - 4 * q) * P
                act.wait_ge(x_flipped, q + 1)
                nc.scalar.copy(xT[0:D, 4 * P * q:4 * P * q + n], flip_ps[q % 2][0:D, 0:n]).then_inc(x_flip_used, 1)
            with act.Fori(0, n_pass) as v:
                with act.Fori(0, STEPS) as i:
                    for u in range(UNROLL):
                        act.wait_ge(feat_ready, v * CHUNKS + i * UNROLL + u + 1)
                        nc.scalar.copy(idx[:, u], e_src[:, i * UNROLL + u]).then_inc(staged, 1)
            for g in range(GROUPS):
                act.wait_ge(centred, g + 1)
                if g:
                    act.wait_ge(var_ready, g)
                nc.scalar.activation(squares[:], h[:, g * GROUP:(g + 1) * GROUP], ACT.Square).then_inc(squared, 1)
            act.wait_ge(var_ready, GROUPS)
            nc.scalar.activation(deg_root[:], var[:], ACT.Sqrt, bias=eps_ln[:], scale=1.0 / D).then_inc(root_ready, 1)

        @block.vector
        def _(dve):
            chain = [0]

            def link(ins):
                chain[0] += 1
                ins.then_inc(dve_chain, 1)
                dve.wait_ge(dve_chain, chain[0])

            nc.vector.memset(row_w[:, 1, :], 0.0).then_inc(pad_w, 1)
            dve.sem_inc(deg_added, DEG_CHUNKS + 1)
            dve.sem_inc(added, 2)
            dve.sem_inc(feat_ready, UNROLL)
            nc.vector.memset(table_sb[:], 0.0).then_inc(pad_x, 1)
            nc.vector.memset(deg_sum[:], 0.0)
            nc.vector.memset(sums[:], 0.0)
            nc.vector.memset(eps_ln[:], EPS)
            link(nc.vector.memset(w_parts[:], 1.0))
            dve.wait_ge(dst_loaded, ROWS_LOADED)
            for g in range(2):
                link(nc.vector.tensor_copy(row_dst[:, g], raw_dst[:, g]))
                nc.vector.tensor_reduce(out=least[:, g:g + 1], in_=row_dst[:, g], axis=AX.X, op=ALU.min)
                link(nc.vector.scalar_tensor_tensor(out=row_real[:], in0=row_dst[:, g], scalar=float(N), in1=row_dst[:, g],
                                                    op0=ALU.is_lt, op1=ALU.mult))
                link(nc.vector.tensor_reduce(out=most[:, g:g + 1], in_=row_real[:], axis=AX.X, op=ALU.max))
            link(nc.vector.tensor_tensor(out=unfit[:], in0=most[:], in1=least[:], op=ALU.subtract))
            link(nc.vector.tensor_scalar(unfit[:], unfit[:], WINDOW - 0.5, None, ALU.is_gt))
            nc.vector.tensor_reduce(out=unfit_any[:], in_=unfit[:], axis=AX.X, op=ALU.max).then_inc(unfit_ready, 1)
            dve.wait_ge(unfit_counted, 1)
            link(nc.vector.tensor_scalar(fits[:], misc_ps[:, 0:1], 0.5, None, ALU.is_lt))
            nc.vector.tensor_scalar(passes[:], fits[0:1, :], 1.0 - WINDOWS, float(WINDOWS), ALU.mult, ALU.add)
            link(nc.vector.tensor_scalar(base[:], least[:], fits[:, 0:1], None, ALU.mult))
            for g, n in groups:
                last = nc.vector.tensor_scalar(row_dst[0:n, g], row_dst[0:n, g], base[0:n, g:g + 1], None, ALU.subtract)
            last.then_inc(base_ready, 1)
            dve.wait_ge(base_flipped, 1)
            nc.vector.tensor_copy(base_row[:], misc_ps[0:1, P:P + CHUNKS]).then_inc(base_stored, 1)
            dve.wait_ge(src_loaded, ROWS_LOADED)
            q = 0
            for k, to in enumerate((e_dst, e_w, e_src)):
                for g, n in groups:
                    if k == 2:
                        nc.vector.tensor_copy(row_src[0:n], raw_src[0:n, g]).then_inc(rows_ready, 1)
                    for half in range(TILES // 4):
                        q += 1
                        dve.wait_ge(flipped, q)
                        nc.vector.tensor_copy(
                            to[:, g * P:g * P + n, 4 * half:4 * half + 4].rearrange("p c j -> p j c"),
                            flip_ps[(q - 1) % 2][:, :].rearrange("p (j c) -> p j c", j=4)[:, :, 0:n]).then_inc(flip_used, 1)
            dve.wait_ge(flip_used, FLIPS)
            flat_w, flat_tmp = (t[:, :, :].rearrange("p c j -> p (c j)") for t in (e_w, e_tmp))
            parts = w_parts[:, :, :, :].rearrange("p c j k -> p (c j) k")
            link(nc.vector.tensor_copy(parts[:, :, 0], flat_w))
            link(nc.vector.tensor_tensor(out=flat_tmp, in0=flat_w, in1=parts[:, :, 0], op=ALU.subtract))
            link(nc.vector.tensor_copy(parts[:, :, 1], flat_tmp))
            nc.vector.tensor_tensor(out=parts[:, :, 2], in0=flat_tmp, in1=parts[:, :, 1], op=ALU.subtract).then_inc(w_split, 1)
            dve.wait_ge(w_split, 1)
            n_pass = dve.value_load(passes[0:1, 0:1], min_val=1, max_val=WINDOWS)

            def window(v, count):
                nc.vector.tensor_scalar(e_tmp[:], e_dst[:], win_off[:, 0:1], -1.0, ALU.subtract, ALU.max).then_inc(pass_step, 1)
                dve.wait_ge(pass_step, count + v * 3 + 1)
                nc.vector.tensor_scalar(e_win[:], e_tmp[:], float(WINDOW), None, ALU.min).then_inc(pass_step, 1)
                nc.vector.tensor_scalar(win_off[:], win_off[:], float(WINDOW), None, ALU.add).then_inc(pass_step, 1)
                dve.wait_ge(pass_step, count + v * 3 + 3)
                dve.sem_inc(windows_set, 1)

            dve.wait_ge(consts, 5)
            link(nc.vector.memset(win_off[:], 0.0))
            with dve.Fori(0, n_pass) as v:
                window(v, 0)
                with dve.Fori(0, STEPS) as i:
                    for s in range(2):
                        step = v * 2 * STEPS + i * 2 + s
                        dve.wait_ge(deg_product, step + 1)
                        tiles = e_win[:, bass.ds(i * UNROLL + s * DEG_CHUNKS, DEG_CHUNKS)].rearrange("p c j -> p (c j)")
                        nc.vector.tensor_tensor(
                            out=hot_b[:, s], in0=tiles.unsqueeze(2).to_broadcast([P, DEG_CHUNKS * TILES, WINDOW]),
                            in1=iota_b[:, :].unsqueeze(1).to_broadcast([P, DEG_CHUNKS * TILES, WINDOW]),
                            op=ALU.is_equal).then_inc(hot_b_ready, 1)
                    for s in range(2):
                        step = v * 2 * STEPS + i * 2 + s
                        dve.wait_ge(deg_product, step + 3)
                        for k in range(DEG_CHUNKS):
                            c = i * UNROLL + s * DEG_CHUNKS + k
                            at = dve.value_load(base_row[0:1, bass.ds(c, 1)], min_val=0, max_val=N - 1)
                            to = deg_sum[:, bass.ds(window_at(at, v), WINDOW)]
                            dve.wait_ge(deg_added, v * CHUNKS + c + DEG_CHUNKS + 1)
                            nc.vector.tensor_tensor(out=to, in0=to, in1=acc_ps[s][0:4, k * WINDOW:(k + 1) * WINDOW],
                                                    op=ALU.add).then_inc(deg_added, 1)
            link(nc.vector.memset(xT[D:D + 1, :], 1.0))
            dve.wait_ge(deg_nodes, 1)
            nc.vector.tensor_scalar(deg_max[:], misc_ps[:, 0:2 * NT].rearrange("p (t k) -> p t k", k=2), 1.0, None,
                                    ALU.max).then_inc(root_in, 1)
            dve.wait_ge(root_in, 1)
            link(nc.vector.reciprocal(inv_count[:], deg_max[:, :, 1]))
            dve.wait_ge(root_out, 1)
            link(nc.vector.reciprocal(inv_root[:], deg_root[:]))
            dve.wait_ge(x_loaded, X_LOADED)
            nc.vector.tensor_copy(table_sb[:, :, D:D + 1], inv_root[:, :].unsqueeze(2)).then_inc(table_ready, 1)

            dve.wait_ge(small_loaded, 16 * 21)
            GCN, SAGE_S, SAGE_N, GIN, GC1, GC2, EDGE = range(7)
            lo, hi = slice(0, D), slice(D, P)

            def scaled(to, of, by):
                return nc.vector.tensor_scalar(to, of, by, None, ALU.mult)

            def plus(to, of, by):
                return nc.vector.scalar_tensor_tensor(out=to, in0=of, scalar=by, in1=to, op0=ALU.mult, op1=ALU.add)

            link(nc.vector.tensor_scalar(gin_scale[:], eps_sb[:], 1.0, mix_sb[:, 2:3], ALU.add, ALU.mult))
            scaled(W_low[lo, 0], W_in[lo, EDGE], mix_sb[lo, 4:5])
            scaled(W_high[hi, 0], W_in[hi, GCN], mix_sb[hi, 0:1])
            scaled(W_high[hi, 1], W_in[hi, SAGE_N], mix_sb[hi, 1:2])
            scaled(W_low[lo, 1], W_in[lo, GIN], mix_sb[lo, 2:3])
            nc.vector.tensor_scalar(W_node[lo], W_in[lo, SAGE_S], mix_sb[lo, 1:2], None, ALU.mult)
            link(scaled(W_node[D:D + 1], b_in[D:D + 1, 0], mix_sb[D:D + 1, 0:1]))
            plus(W_low[lo, 1], W_in[lo, GC2], mix_sb[lo, 3:4])
            plus(W_node[lo], W_in[lo, GIN], gin_scale[lo])
            link(plus(W_node[D:D + 1], b_in[D:D + 1, 1], mix_sb[D:D + 1, 1:2]))
            plus(W_node[lo], W_in[lo, GC1], mix_sb[lo, 3:4])
            link(plus(W_node[D:D + 1], b_in[D:D + 1, 2], mix_sb[D:D + 1, 2:3]))
            nc.vector.tensor_tensor(out=W_node[lo], in0=W_node[lo], in1=ident[lo, 0:D], op=ALU.add)
            link(plus(W_node[D:D + 1], b_in[D:D + 1, 3], mix_sb[D:D + 1, 3:4]))
            link(plus(W_node[D:D + 1], b_in[D:D + 1, 4], mix_sb[D:D + 1, 4:5]))
            dve.sem_inc(weights_mixed, 1)

            link(nc.vector.memset(win_off[:], 0.0))
            with dve.Fori(0, n_pass) as v:
                window(v, n_pass * 3)
                with dve.Fori(0, STEPS) as i:

                    def features(u):
                        c = i * UNROLL + u
                        it = v * CHUNKS + c
                        turn = v * STEPS + i + 1
                        w = e_w[:, c].unsqueeze(2).to_broadcast([P, TILES, D])
                        dve.wait_ge(chunk_product, it + 1)
                        nc.vector.tensor_tensor(
                            out=hot[:, u], in0=e_win[:, c].unsqueeze(2).to_broadcast([P, TILES, WINDOW]),
                            in1=iota_b[:, :].unsqueeze(1).to_broadcast([P, TILES, WINDOW]), op=ALU.is_equal)
                        dve.wait_ge(gathered[u], turn * (16 * TILES))
                        xs = feat[:, u, :, 3 * D:4 * D]
                        nc.vector.tensor_tensor(out=wroot[:, u], in0=e_w[:, c], in1=feat[:, u, :, 4 * D],
                                                op=ALU.mult).then_inc(wroot_ready, 1)
                        dve.wait_ge(attr_loaded[u], turn * 16)
                        nc.vector.tensor_tensor(out=attr[:, u], in0=attr[:, u], in1=xs, op=ALU.add).then_inc(summed_in, 1)
                        nc.vector.tensor_tensor(out=feat[:, u, :, 2 * D:3 * D], in0=xs, in1=w, op=ALU.mult)
                        dve.wait_ge(wroot_ready, it + 1)
                        nc.vector.tensor_tensor(out=feat[:, u, :, D:2 * D], in0=xs,
                                                in1=wroot[:, u].unsqueeze(2).to_broadcast([P, TILES, D]), op=ALU.mult)
                        dve.wait_ge(summed_in, it + 1)
                        nc.vector.scalar_tensor_tensor(out=feat[:, u, :, 0:D], in0=attr[:, u], scalar=0.0, in1=w,
                                                       op0=ALU.max, op1=ALU.mult).then_inc(feat_ready, 1)

                    def add(u):
                        c = i * UNROLL + u
                        it = v * CHUNKS + c
                        at = dve.value_load(base_row[0:1, bass.ds(c, 1)], min_val=0, max_val=N - 1)
                        to = sums[:, :, bass.ds(window_at(at, v), WINDOW)]
                        dve.wait_ge(chunk_product, it + 1 + UNROLL)
                        dve.wait_ge(added, it + 2)
                        nc.vector.tensor_tensor(out=to, in0=to, in1=acc_ps[u % 2][:, 0:2 * WINDOW].rearrange(
                            "p (k n) -> p k n", k=2), op=ALU.add).then_inc(added, 1)

                    for u in range(UNROLL):
                        features(u)
                        if u:
                            add(u - 1)
                    add(UNROLL - 1)

            for g in range(GROUPS):
                tiles = slice(g * GROUP, (g + 1) * GROUP)
                cols = GROUP * D

                def per_node(t):
                    return t[:, tiles].unsqueeze(2).to_broadcast([P, GROUP, D])

                def ps(t):
                    return t[:, 0:cols].rearrange("p (t d) -> p t d", d=D)

                dve.wait_ge(out_product, g + 1)
                nc.vector.tensor_tensor(out=h_tmp[:, 0], in0=ps(gcn_ps), in1=per_node(inv_root), op=ALU.mult)
                link(nc.vector.tensor_tensor(out=h_tmp[:, 1], in0=ps(sage_ps), in1=per_node(inv_count), op=ALU.mult))
                link(nc.vector.tensor_tensor(out=h_tmp[:, 0], in0=h_tmp[:, 0], in1=h_tmp[:, 1], op=ALU.add))
                nc.vector.tensor_tensor(out=h[:, tiles], in0=ps(node_ps), in1=h_tmp[:, 0], op=ALU.add).then_inc(out_taken, 1)
                dve.wait_ge(out_taken, g + 1)
                link(nc.vector.tensor_reduce(out=mean[:, tiles], in_=h[:, tiles], axis=AX.X, op=ALU.add))
                link(nc.vector.tensor_scalar(mean[:, tiles], mean[:, tiles], 1.0 / D, None, ALU.mult))
                nc.vector.tensor_tensor(out=h[:, tiles], in0=h[:, tiles], in1=per_node(mean), op=ALU.subtract).then_inc(centred, 1)
                dve.wait_ge(squared, g + 1)
                nc.vector.tensor_reduce(out=var[:, tiles], in_=squares[:], axis=AX.X, op=ALU.add).then_inc(var_ready, 1)
            dve.wait_ge(root_ready, 1)
            link(nc.vector.reciprocal(var[:], deg_root[:]))
            for g in range(GROUPS):
                tiles = slice(g * GROUP, (g + 1) * GROUP)
                nc.vector.tensor_tensor(out=h[:, tiles], in0=h[:, tiles],
                                        in1=var[:, tiles].unsqueeze(2).to_broadcast([P, GROUP, D]),
                                        op=ALU.mult).then_inc(out_ready, 1)

        @block.tensor
        def _(pe):
            pe.sem_inc(chunk_product, UNROLL)
            pe.wait_ge(consts, 5)
            pe.wait_ge(unfit_ready, 1)
            nc.tensor.matmul(misc_ps[:, 0:1], ones[:], unfit_any[:], start=True, stop=True).then_inc(unfit_counted, 1)
            pe.wait_ge(base_ready, 1)
            for g, n in groups:
                last = nc.tensor.transpose(misc_ps[0:1, P + g * P:P + g * P + n], base[0:n, g:g + 1], ident[0:n, 0:n])
            last.then_inc(base_flipped, 1)
            q = 0
            for k, rows in enumerate((row_dst, row_w, row_src)):
                if k == 1:
                    pe.wait_ge(w_loaded, ROWS_LOADED)
                for g, n in groups:
                    if k == 2:
                        pe.wait_ge(rows_ready, g + 1)
                    v = (rows[:, g] if k < 2 else rows[:, :]).rearrange("c (p j) -> c j p", j=TILES)
                    for half in range(TILES // 4):
                        q += 1
                        if q > 2:
                            pe.wait_ge(flip_used, q - 2)
                        for j in range(4):
                            last = nc.tensor.transpose(flip_ps[(q - 1) % 2][:, j * P:j * P + n],
                                                       v[0:n, 4 * half + j], ident[0:n, 0:n])
                        last.then_inc(flipped, 1)
            pe.wait_ge(base_stored, 1)
            n_pass = pe.value_load(passes[0:1, 0:1], min_val=1, max_val=WINDOWS)
            pe.sem_inc(deg_product, 2)
            with pe.Fori(0, n_pass) as v:
                with pe.Fori(0, STEPS) as i:
                    for s in range(2):
                        step = v * 2 * STEPS + i * 2 + s
                        pe.wait_ge(hot_b_ready, step + 1)
                        pe.wait_ge(w_staged, step + 1)
                        pe.wait_ge(deg_added, step * DEG_CHUNKS + 1)
                        for k in range(DEG_CHUNKS):
                            for j in range(TILES):
                                last = nc.tensor.matmul(acc_ps[s][0:4, k * WINDOW:(k + 1) * WINDOW], w_stage[:, s, k, j],
                                                        hot_b[:, s, k * TILES + j], start=(j == 0), stop=(j == TILES - 1))
                        last.then_inc(deg_product, 1)
            pe.wait_ge(deg_added, n_pass * CHUNKS + DEG_CHUNKS + 1)
            for t in range(NT):
                last = nc.tensor.matmul(misc_ps[:, 2 * t:2 * t + 2], deg_sum[:, t:t + (P - 1) * NT + 1:NT], part_sel[:, :],
                                        start=True, stop=True)
            last.then_inc(deg_nodes, 1)
            pe.wait_ge(x_loaded, X_LOADED)
            pe.wait_ge(flip_used, FLIPS)
            for q in range(XFLIPS):
                if q >= 2:
                    pe.wait_ge(x_flip_used, q - 1)
                for t in range(4 * q, min(4 * q + 4, NT)):
                    last = nc.tensor.transpose(flip_ps[q % 2][0:D, (t % 4) * P:(t % 4 + 1) * P], table_sb[:, t, 0:D], ident[:])
                last.then_inc(x_flipped, 1)
            with pe.Fori(0, n_pass) as v:
                with pe.Fori(0, STEPS) as i:
                    for u in range(UNROLL):
                        it = v * CHUNKS + i * UNROLL + u
                        pe.wait_ge(feat_ready, it + 1 + UNROLL)
                        pe.wait_ge(added, it + 1)
                        for k in range(2):
                            for j in range(TILES):
                                last = nc.tensor.matmul(acc_ps[u % 2][:, k * WINDOW:(k + 1) * WINDOW],
                                                        feat[:, u, j, 2 * D * k:2 * D * (k + 1)], hot[:, u, j],
                                                        start=(j == 0), stop=(j == TILES - 1))
                        last.then_inc(chunk_product, 1)
            pe.wait_ge(added, n_pass * CHUNKS + 2)
            pe.wait_ge(weights_mixed, 1)
            pe.wait_ge(x_flip_used, XFLIPS)
            for g in range(GROUPS):
                if g:
                    pe.wait_ge(out_taken, g)
                for n in range(GROUP):
                    t, to = g * GROUP + n, slice(n * D, (n + 1) * D)
                    nodes = slice(t, t + (P - 1) * NT + 1, NT)
                    nc.tensor.matmul(node_ps[:, to], sums[0:D, 0, nodes], W_low[0:D, 0], start=True, stop=False)
                    nc.tensor.matmul(node_ps[:, to], sums[0:D, 1, nodes], W_low[0:D, 1], start=False, stop=False)
                    nc.tensor.matmul(node_ps[:, to], xT[:, t * P:(t + 1) * P], W_node[:, :], start=False, stop=True)
                    nc.tensor.matmul(gcn_ps[:, to], sums[D:P, 0, nodes], W_high[D:P, 0], start=True, stop=True)
                    last = nc.tensor.matmul(sage_ps[:, to], sums[D:P, 1, nodes], W_high[D:P, 1], start=True, stop=True)
                last.then_inc(out_product, 1)


INPUTS = ("x", "src", "dst", "edge_attr_64", "edge_weight", "L0_gnn_weights", "L0_gnn_Wgcn", "L0_gnn_bgcn",
          "L0_gnn_Wsage_s", "L0_gnn_Wsage_n", "L0_gnn_bsage", "L0_gnn_gin_eps", "L0_gnn_Wgin", "L0_gnn_bgin",
          "L0_gnn_Wgc1", "L0_gnn_Wgc2", "L0_gnn_bgc", "L0_gnn_Wedge", "L0_gnn_bedge")


def kernel(**inputs):
    import concourse.bacc as bacc
    from concourse.bass_utils import run_bass_kernel_spmd

    nc = bacc.Bacc("TRN2", target_bir_lowering=False, num_devices=1)
    arrays, args = {}, []
    for name in INPUTS:
        a = np.ascontiguousarray(inputs[name])
        if a.ndim == 0 or name.endswith("gin_eps"):
            a = a.reshape(1, 1)
        arrays[f"in_{name}"] = a
        args.append(nc.dram_tensor(f"in_{name}", a.shape, mybir.dt.from_np(a.dtype), kind="ExternalInput").ap())
    out = nc.dram_tensor("out", (N, D), F32, kind="ExternalOutput").ap()
    build(nc, *args, out)
    return run_bass_kernel_spmd(nc, [arrays], core_ids=[0]).results[0]["out"]
```

```python
from contextlib import ExitStack

import concourse.bass as bass
import numpy as np
from concourse import mybir

F32 = mybir.dt.float32
BF16 = mybir.dt.bfloat16
I32 = mybir.dt.int32
U32 = mybir.dt.uint32
ALU = mybir.AluOpType
ACT = mybir.ActivationFunctionType
AX = mybir.AxisListType

P = 128
N, D = 6250, 64
E = 200000
TILES = 8
CHUNK = P * TILES
CHUNKS = -(-E // CHUNK)
LAST_START = E - CHUNK
LAST_OLD = (CHUNKS - 1) * CHUNK - LAST_START
UNROLL = 4
STEPS = CHUNKS // UNROLL
WINDOW = 48
WINDOWS = -(-N // WINDOW)
NT = -(-N // P)
NPAD = P * NT
SUMS = NPAD + WINDOW
TROW = D + 4
BLOCK = 3 * D + TROW
DEG_CHUNKS = 2
DEG_SLOTS = 4
FAR = 1.0e6
EPS = 1e-5
GROUP = 7
assert CHUNKS == STEPS * UNROLL and NT % GROUP == 0 and UNROLL == 2 * DEG_CHUNKS


def build(nc, x, src, dst, edge_attr, edge_weight, mix, Wgcn, bgcn, Wsage_s, Wsage_n, bsage,
          gin_eps, Wgin, bgin, Wgc1, Wgc2, bgc, Wedge, bedge, out):
    ctx = ExitStack()
    with ctx:
        def sb(name, shape, dt=F32):
            return ctx.enter_context(nc.sbuf_tensor(name, shape, dt))

        def pb(name, shape):
            return ctx.enter_context(nc.psum_tensor(name, shape, F32))

        def sem(name):
            return ctx.enter_context(nc.semaphore(name))

        table = nc.dram_tensor("node_table", [NPAD, TROW], F32, kind="Internal").ap()

        LOW, HIGH = P, CHUNKS - P
        groups = ((0, P), (1, HIGH))
        area = sb("area", [P, NPAD])
        raw_src, raw_dst = (area[:, k * 2 * CHUNK:(k + 1) * 2 * CHUNK].bitcast(I32).rearrange("p (g e) -> p g e", g=2)
                            for k in range(2))
        row_src = area[:, 0:2 * CHUNK].rearrange("p (g e) -> p g e", g=2)
        row_w = area[:, 4 * CHUNK:6 * CHUNK].rearrange("p (g e) -> p g e", g=2)
        attr = sb("attr", [P, UNROLL, TILES, D])
        feat = sb("feat", [P, UNROLL, TILES, BLOCK])
        attr_flat, feat_flat = (t[:, :, :, :].rearrange("p u j b -> p (u j b)") for t in (attr, feat))
        hot = sb("hot", [P, UNROLL, TILES, WINDOW])
        row_far = hot[:, :, :, :].rearrange("p u j n -> p (u j n)")[:, 0:CHUNK]
        row_dst = attr_flat[:, 0:2 * CHUNK].rearrange("p (g e) -> p g e", g=2)
        least = sb("least", [P, 2])
        most = sb("most", [P, 2])
        unfit = sb("unfit", [P, 2])
        unfit_any = sb("unfit_any", [P, 1])
        fits = sb("fits", [P, 1])
        base = sb("base", [P, 2])
        base_row = sb("base_row", [1, CHUNKS], I32)
        passes = sb("passes", [1, 1], I32)
        e_src = sb("e_src", [P, CHUNKS + UNROLL, TILES], U32)
        e_dst = sb("e_dst", [P, CHUNKS, TILES])
        e_win = sb("e_win", [P, CHUNKS, TILES], BF16)
        e_tmp = sb("e_tmp", [P, CHUNKS, TILES])
        e_w = sb("e_w", [P, CHUNKS, TILES])
        w_parts = sb("w_parts", [P, CHUNKS, TILES, 4], BF16)
        ident = sb("ident", [P, P])
        ones = sb("ones", [P, P])
        iota_b = sb("iota_b", [P, WINDOW], BF16)
        iota_t = sb("iota_t", [P, WINDOW, DEG_CHUNKS * TILES], BF16)
        win_off = sb("win_off", [P, 1])
        w_stage = sb("w_stage", [P, DEG_SLOTS, DEG_CHUNKS, TILES, 4], BF16)
        hot_b = sb("hot_b", [P, DEG_SLOTS, WINDOW, DEG_CHUNKS * TILES], BF16)
        deg_sum = feat_flat[:, 0:SUMS]
        deg_node = sb("deg_node", [P, 2 * 4, NT])
        deg_max = sb("deg_max", [P, NT, 2])
        deg_root = sb("deg_root", [P, NT])
        inv_root = sb("inv_root", [P, NT])
        inv_count = sb("inv_count", [P, NT])
        table_sb = sb("table_sb", [P, NT, TROW])
        idx = sb("idx", [P, UNROLL, TILES], U32)
        wroot = sb("wroot", [P, UNROLL, TILES])
        sums = sb("sums", [P, 2, SUMS])
        xT = area[0:D + 1, :]
        W_in = sb("W_in", [P, 7, D])
        b_in = sb("b_in", [D + 1, 5, D])
        mix_sb = sb("mix_sb", [P, 5])
        eps_sb = sb("eps_sb", [P, 1])
        eps_ln = sb("eps_ln", [P, 1])
        gin_scale = sb("gin_scale", [P, 1])
        W_node = sb("W_node", [D + 1, D])
        W_pair = sb("W_pair", [P, 2, 2, D])
        h_node = sb("h_node", [P, NT, D])
        h = feat_flat[:, 0:NT * D].rearrange("p (t d) -> p t d", d=D)
        h_tmp = feat_flat[:, NT * D:(NT + 4 * GROUP) * D].rearrange("p (k t d) -> p k t d", k=4, d=D)
        squares = attr_flat[:, 0:2 * GROUP * D].rearrange("p (s t d) -> p s t d", s=2, d=D)
        mean = sb("mean", [P, NT])
        var = sb("var", [P, NT])

        psum = pb("psum", [P, 8 * 512])
        bank = [psum[:, k * 512:(k + 1) * 512] for k in range(8)]
        acc_ps, flip_ps, misc_ps, node_ps, deg_ps = bank[0:2], bank[2:4], bank[4], bank[5:7], bank[0:2] + bank[5:7]
        pair_ps = psum[:, :].rearrange("p (s k t c) -> p s k t c", s=2, k=2, c=2 * D)

        dst_loaded, src_loaded, w_loaded = sem("dst_loaded"), sem("src_loaded"), sem("w_loaded")
        far_ready, pad_x, zeroed = sem("far_ready"), sem("pad_x"), sem("zeroed")
        x_loaded, small_loaded = sem("x_loaded"), sem("small_loaded")
        consts = sem("consts")
        gathers_begun, windows_set = sem("gathers_begun"), sem("windows_set")
        dve_chain, pass_step = sem("dve_chain"), sem("pass_step")
        pool_chain = sem("pool_chain")
        unfit_ready, unfit_counted = sem("unfit_ready"), sem("unfit_counted")
        base_ready, base_flipped, base_stored = sem("base_ready"), sem("base_flipped"), sem("base_stored")
        rows_ready, flipped, flip_used = sem("rows_ready"), sem("flipped"), sem("flip_used")
        dst_flip_used = sem("dst_flip_used")
        w_high, w_split = sem("w_high"), sem("w_split")
        w_staged, src_wrapped = sem("w_staged"), sem("src_wrapped")
        deg_summed, deg_turned = sem("deg_summed"), sem("deg_turned")
        hot_b_ready, deg_product, deg_added = sem("hot_b_ready"), sem("deg_product"), sem("deg_added")
        root_in, root_out = sem("root_in"), sem("root_out")
        table_ready, table_stored = sem("table_ready"), sem("table_stored")
        x_flipped, x_flip_used = sem("x_flipped"), sem("x_flip_used")
        node_product, node_taken = sem("node_product"), sem("node_taken")
        staged = sem("staged")
        gathered = [sem(f"gathered{u}") for u in range(UNROLL)]
        attr_loaded = [sem(f"attr_loaded{u}") for u in range(UNROLL)]
        wroot_ready, summed_in = sem("wroot_ready"), sem("summed_in")
        feat_ready = sem("feat_ready")
        chunk_product = sem("chunk_product")
        added = sem("added")
        weights_mixed = sem("weights_mixed")
        out_product, out_taken = sem("out_product"), sem("out_taken")
        centred, squared, var_ready, root_ready = sem("centred"), sem("squared"), sem("var_ready"), sem("root_ready")
        out_ready, stored = sem("out_ready"), sem("stored")

        FLIPS = 3 * 2 * (TILES // 4)
        DST_FLIPS = FLIPS // 3
        XFLIPS = -(-NT // 4)
        GROUPS = NT // GROUP

        block = ctx.enter_context(nc.Block())

        flat_w, flat_tmp = (t[:, :, :].rearrange("p c j -> p (c j)") for t in (e_w, e_tmp))
        parts = w_parts[:, :, :, :].rearrange("p c j k -> p (c j) k")

        def flip_place(t, g, n, half):
            return t[:, g * P:g * P + n, 4 * half:4 * half + 4].rearrange("p c j -> p j c")

        def flip_of(q, n):
            return flip_ps[(q - 1) % 2].rearrange("p (j c) -> p j c", j=4)[:, :, 0:n]

        def first_windows(eng, i):
            return nc.values_load_multi_w_load_instructions(
                base_row[0:1, bass.ds(i * UNROLL, UNROLL)], engines=(eng.engine,), min_val=0, max_val=N - 1,
                skip_runtime_bounds_check_because="destinations are nodes")[1]

        def window_at(first, v):
            return nc.s_assert_within(first + v * WINDOW, 0, NPAD,
                                      skip_runtime_bounds_check_because="first is 0 in all passes but the first")

        def rows_of(t, c0, c1):
            return t[c0 * CHUNK:c1 * CHUNK].rearrange("(c e) -> c e", e=CHUNK)

        def load_rows(eng, t, rows, loaded):
            eng.dma_start(rows[:, 0, :], rows_of(t, 0, P)).then_inc(loaded, 16)
            full = CHUNKS - 1 - P
            cut = full - full % 16
            eng.dma_start(rows[0:cut, 1, :], rows_of(t, P, P + cut)).then_inc(loaded, 16)
            eng.dma_start(rows[cut:full, 1, :], rows_of(t, P + cut, P + full)).then_inc(loaded, 16)
            eng.dma_start(rows[full:full + 1, 1, :],
                          t[LAST_START:E].rearrange("(a e) -> a e", a=1)).then_inc(loaded, 16)

        ROWS_LOADED = 4 * 16

        def node_rows(t, rows):
            full = N // NT
            cut = full - full % 16
            v = t[0:full * NT, :].rearrange("(p t) d -> p t d", t=NT)
            rest = N - full * NT
            return ((v[0:cut], rows[0:cut]), (v[cut:full], rows[cut:full]),
                    (t[full * NT:N, :].rearrange("(p t) d -> p t d", p=1), rows[full:full + 1, 0:rest]))

        X_LOADED = 3 * 16

        @block.sync
        def _(sp):
            load_rows(sp, dst, raw_dst, dst_loaded)
            load_rows(sp, src, raw_src, src_loaded)
            sp.wait_ge(pad_x, 1)
            for of, to in node_rows(x, table_sb[:, :, 0:D]):
                sp.dma_start(to, of).then_inc(x_loaded, 16)
            sp.wait_ge(deg_summed, 1)
            for k in range(DEG_CHUNKS):
                for part in range(4):
                    row = 32 * k + part
                    sp.dma_start(deg_node[:, 4 * k + part, :],
                                 deg_sum[row:row + 1, 0:NPAD].rearrange("k (p t) -> k p t", t=NT)).then_inc(deg_turned, 16)
            sp.wait_ge(table_ready, 1)
            sp.dma_start(table.rearrange("(p t) d -> p (t d)", p=P),
                         table_sb[:, :, :].rearrange("p t d -> p (t d)")).then_inc(table_stored, 16)
            sp.wait_ge(base_stored, 1)
            n_pass = sp.value_load(passes[0:1, 0:1], min_val=1, max_val=WINDOWS)
            with sp.Fori(0, n_pass) as v:
                with sp.Fori(0, STEPS) as i:
                    for u in range(UNROLL):
                        c = i * UNROLL + u
                        start = c * CHUNK
                        if u == UNROLL - 1:
                            start = nc.s_assert_within(start - (c // (CHUNKS - 1)) * ((CHUNKS - 1) * CHUNK - LAST_START),
                                                       min_val=0, max_val=LAST_START,
                                                       skip_runtime_bounds_check_because="the last chunk is moved back")
                        sp.wait_ge(feat_ready, v * CHUNKS + c + 1)
                        sp.dma_start(attr[:, u, :, :].rearrange("p j d -> p (j d)"),
                                     edge_attr[bass.ds(start, CHUNK), :].rearrange(
                                         "(p j) d -> p (j d)", p=P)).then_inc(attr_loaded[u], 16)
            full, rest = N // NT, N % NT
            cut, n_out = full - full % 16, 0
            of_full = out[0:full * NT, :].rearrange("(p t) d -> p t d", t=NT)
            of_last = out[full * NT:N, :].rearrange("(p t) d -> p t d", p=1)
            for g in range(GROUPS):
                sp.wait_ge(out_ready, g + 1)
                t0, t1 = g * GROUP, (g + 1) * GROUP
                for p0, p1 in ((0, cut), (cut, full)):
                    sp.dma_start(of_full[p0:p1, t0:t1], h[p0:p1, t0:t1]).then_inc(stored, 16)
                    n_out += 1
                if t0 < rest:
                    sp.dma_start(of_last[:, t0:min(t1, rest)], h[full:full + 1, t0:min(t1, rest)]).then_inc(stored, 16)
                    n_out += 1
            sp.wait_ge(stored, 16 * n_out)

        @block.gpsimd
        def _(pool):
            nc.gpsimd.memset(table_sb[:], 0.0).then_inc(pad_x, 1)
            nc.gpsimd.memset(row_far[:], 0.0).then_inc(pool_chain, 1)
            pool.wait_ge(pool_chain, 1)
            nc.gpsimd.affine_select(out=row_far[:, 0:LAST_OLD], in_=row_far[:, 0:LAST_OLD], compare_op=ALU.not_equal,
                                    fill=FAR, base=-(HIGH - 1), pattern=[[0, LAST_OLD]],
                                    channel_multiplier=1).then_inc(far_ready, 1)
            nc.gpsimd.iota(iota_b[:], [[1, WINDOW]], base=0, channel_multiplier=0,
                           allow_small_or_imprecise_dtypes=True).then_inc(consts, 1)
            nc.gpsimd.iota(iota_t[:], [[1, WINDOW], [0, DEG_CHUNKS * TILES]], base=0, channel_multiplier=0,
                           allow_small_or_imprecise_dtypes=True).then_inc(consts, 1)
            nc.gpsimd.memset(ident[:], 0.0).then_inc(pool_chain, 1)
            nc.gpsimd.memset(ones[:], 1.0).then_inc(consts, 1)
            pool.wait_ge(pool_chain, 2)
            nc.gpsimd.affine_select(out=ident[:], in_=ident[:], compare_op=ALU.not_equal, fill=1.0, base=0,
                                    pattern=[[-1, P]], channel_multiplier=1).then_inc(consts, 1)
            nc.gpsimd.memset(w_parts[:, :, :, 3:4], 1.0).then_inc(zeroed, 1)
            nc.gpsimd.memset(deg_sum[:], 0.0).then_inc(zeroed, 1)
            nc.gpsimd.memset(sums[:], 0.0).then_inc(zeroed, 1)
            nc.gpsimd.memset(W_pair[:], 0.0).then_inc(zeroed, 1)
            pool.wait_ge(table_stored, 16)
            pool.wait_ge(base_stored, 1)
            n_pass = pool.value_load(passes[0:1, 0:1], min_val=1, max_val=WINDOWS)
            with pool.Fori(0, n_pass) as v:
                with pool.Fori(0, STEPS) as i:
                    for u in range(UNROLL):
                        it = v * CHUNKS + i * UNROLL + u
                        pool.wait_ge(staged, it + 1)
                        pool.wait_ge(chunk_product, it + 1)
                        pool.sem_inc(gathers_begun, 1)
                        for j in range(TILES):
                            nc.gpsimd.indirect_dma_start(
                                out=feat[:, u, j, 3 * D:BLOCK], out_offset=None, in_=table,
                                in_offset=bass.IndirectOffsetOnAxis(ap=idx[:, u, j:j + 1], axis=0),
                            ).then_inc(gathered[u], 16)

        @block.scalar
        def _(act):
            load_rows(act, edge_weight, row_w, w_loaded)
            for k, W in enumerate((Wgcn, Wsage_s, Wsage_n, Wgin, Wgc1, Wgc2, Wedge)):
                for half in range(2):
                    act.dma_start(W_in[half * D:(half + 1) * D, k, :], W).then_inc(small_loaded, 16)
            for k, b in enumerate((bgcn, bsage, bgin, bgc, bedge)):
                act.dma_start(b_in[D:D + 1, k, :], b.rearrange("(a d) -> a d", a=1)).then_inc(small_loaded, 16)
            act.dma_start(mix_sb[:, :], mix.rearrange("(a k) -> a k", a=1).to_broadcast([P, 5])).then_inc(small_loaded, 16)
            act.dma_start(eps_sb[:, :], gin_eps.to_broadcast([P, 1])).then_inc(small_loaded, 16)

            q = DST_FLIPS
            for to in (e_w, e_src):
                if to is e_src:
                    act.wait_ge(src_loaded, ROWS_LOADED)
                    for g, n in groups:
                        nc.scalar.copy(row_src[0:n, g], raw_src[0:n, g]).then_inc(rows_ready, 1)
                for g, n in groups:
                    for half in range(TILES // 4):
                        q += 1
                        act.wait_ge(flipped, q)
                        nc.scalar.copy(flip_place(to, g, n, half), flip_of(q, n)).then_inc(flip_used, 1)
                if to is e_w:
                    act.wait_ge(flip_used, q - DST_FLIPS)
                    nc.scalar.copy(parts[:, :, 0], flat_w).then_inc(w_high, 1)
            act.wait_ge(flip_used, FLIPS - DST_FLIPS)
            nc.scalar.copy(idx[:, :, :], e_src[:, 0:UNROLL]).then_inc(staged, UNROLL)
            nc.scalar.copy(e_src[:, CHUNKS:CHUNKS + UNROLL], e_src[:, 0:UNROLL]).then_inc(src_wrapped, 1)
            act.wait_ge(src_wrapped, 1)
            act.wait_ge(base_stored, 1)
            n_pass = act.value_load(passes[0:1, 0:1], min_val=1, max_val=WINDOWS)
            act.wait_ge(w_split, 1)
            act.wait_ge(zeroed, 1)
            with act.Fori(0, n_pass) as v:
                act.wait_ge(deg_product, v * 2 * STEPS + DEG_SLOTS)

                def stage_weights(i, half):
                    for s in range(2):
                        act.wait_ge(deg_product, v * 2 * STEPS + i * 2 + s + 1)
                        nc.scalar.copy(w_stage[:, 2 * half + s],
                                       w_parts[:, bass.ds(i * UNROLL + s * DEG_CHUNKS, DEG_CHUNKS)]).then_inc(w_staged, 1)

                with act.Fori(0, STEPS // 2) as i2:
                    stage_weights(i2 * 2, 0)
                    stage_weights(i2 * 2 + 1, 1)
                stage_weights(STEPS - 1, 0)
            act.wait_ge(root_in, 1)
            nc.scalar.activation(deg_root[:], deg_max[:, :, 0], ACT.Sqrt).then_inc(root_out, 1)
            for q in range(XFLIPS):
                n = min(4, NT - 4 * q) * P
                act.wait_ge(x_flipped, q + 1)
                nc.scalar.copy(xT[0:D, 4 * P * q:4 * P * q + n], flip_ps[q % 2][0:D, 0:n]).then_inc(x_flip_used, 1)
            for g in range(GROUPS):
                act.wait_ge(node_product, g + 1)
                nc.scalar.copy(h_node[:, g * GROUP:(g + 1) * GROUP],
                               node_ps[g % 2][:, 0:GROUP * D].rearrange("p (t d) -> p t d", d=D)).then_inc(node_taken, 1)
            with act.Fori(0, n_pass) as v:
                with act.Fori(0, STEPS) as i:
                    for u in range(UNROLL):
                        act.wait_ge(gathered[u], (v * STEPS + i + 1) * (16 * TILES))
                        nc.scalar.copy(idx[:, u], e_src[:, (i + 1) * UNROLL + u]).then_inc(staged, 1)
            for g in range(GROUPS):
                tiles = slice(g * GROUP, (g + 1) * GROUP)
                act.wait_ge(centred, g + 1)
                nc.scalar.activation(squares[:, g % 2], h[:, tiles], ACT.Square).then_inc(squared, 1)
                act.wait_ge(var_ready, g + 1)
                nc.scalar.activation(deg_root[:, tiles], var[:, tiles], ACT.Sqrt, bias=eps_ln[:], scale=1.0 / D
                                     ).then_inc(root_ready, 1)

        @block.vector
        def _(dve):
            chain = [0]

            def link(ins):
                chain[0] += 1
                ins.then_inc(dve_chain, 1)
                dve.wait_ge(dve_chain, chain[0])

            dve.sem_inc(deg_added, DEG_SLOTS * DEG_CHUNKS)
            dve.sem_inc(added, 2)
            dve.sem_inc(feat_ready, UNROLL)
            nc.vector.memset(eps_ln[:], EPS)
            nc.vector.memset(least[:], 0.0)
            link(nc.vector.memset(most[:], 0.0))
            dve.wait_ge(dst_loaded, ROWS_LOADED)
            for g, n in groups:
                nc.vector.tensor_reduce(out=least[0:n, g:g + 1], in_=raw_dst[0:n, g], axis=AX.X, op=ALU.min)
                last = nc.vector.tensor_reduce(out=most[0:n, g:g + 1], in_=raw_dst[0:n, g], axis=AX.X, op=ALU.max)
            link(last)
            link(nc.vector.tensor_tensor(out=unfit[:], in0=most[:], in1=least[:], op=ALU.subtract))
            link(nc.vector.tensor_scalar(unfit[:], unfit[:], WINDOW - 0.5, None, ALU.is_gt))
            nc.vector.tensor_reduce(out=unfit_any[:], in_=unfit[:], axis=AX.X, op=ALU.max).then_inc(unfit_ready, 1)
            dve.wait_ge(unfit_counted, 1)
            link(nc.vector.tensor_scalar(fits[:], misc_ps[:, 0:1], 0.5, None, ALU.is_lt))
            nc.vector.tensor_scalar(passes[:], fits[0:1, :], 1.0 - WINDOWS, float(WINDOWS), ALU.mult, ALU.add)
            link(nc.vector.tensor_scalar(base[:], least[:], fits[:, 0:1], None, ALU.mult))
            nc.vector.tensor_scalar(row_dst[:, 0], raw_dst[:, 0], base[:, 0:1], None, ALU.subtract)
            dve.wait_ge(far_ready, 1)
            nc.vector.scalar_tensor_tensor(out=row_dst[0:HIGH, 1], in0=raw_dst[0:HIGH, 1], scalar=base[0:HIGH, 1:2],
                                           in1=row_far[0:HIGH], op0=ALU.subtract, op1=ALU.add).then_inc(base_ready, 1)
            dve.wait_ge(base_flipped, 1)
            nc.vector.tensor_copy(base_row[:], misc_ps[0:1, P:P + CHUNKS]).then_inc(base_stored, 1)
            q = 0
            for g, n in groups:
                for half in range(TILES // 4):
                    q += 1
                    dve.wait_ge(flipped, q)
                    nc.vector.tensor_copy(flip_place(e_dst, g, n, half), flip_of(q, n)).then_inc(dst_flip_used, 1)
            dve.wait_ge(dst_flip_used, DST_FLIPS)
            dve.wait_ge(w_high, 1)
            link(nc.vector.tensor_tensor(out=flat_tmp, in0=flat_w, in1=parts[:, :, 0], op=ALU.subtract))
            link(nc.vector.tensor_copy(parts[:, :, 1], flat_tmp))
            nc.vector.tensor_tensor(out=parts[:, :, 2], in0=flat_tmp, in1=parts[:, :, 1], op=ALU.subtract).then_inc(w_split, 1)
            dve.wait_ge(w_split, 1)
            n_pass = dve.value_load(passes[0:1, 0:1], min_val=1, max_val=WINDOWS)

            def window(v, count):
                nc.vector.tensor_scalar(e_tmp[:], e_dst[:], win_off[:, 0:1], -1.0, ALU.subtract, ALU.max).then_inc(pass_step, 1)
                dve.wait_ge(pass_step, count + v * 3 + 1)
                nc.vector.tensor_scalar(e_win[:], e_tmp[:], float(WINDOW), None, ALU.min).then_inc(pass_step, 1)
                nc.vector.tensor_scalar(win_off[:], win_off[:], float(WINDOW), None, ALU.add).then_inc(pass_step, 1)
                dve.wait_ge(pass_step, count + v * 3 + 3)
                dve.sem_inc(windows_set, 1)

            dve.wait_ge(consts, 4)
            link(nc.vector.memset(win_off[:], 0.0))
            dve.wait_ge(zeroed, 2)
            with dve.Fori(0, n_pass) as v:
                window(v, 0)
                def one_hots(i, half):
                    before = dve.snap(v * 2 * STEPS + i * 2)
                    for s in range(2):
                        slot = 2 * half + s
                        dve.wait_ge(deg_product, before + (s + 1))
                        tiles = e_win[:, bass.ds(i * UNROLL + s * DEG_CHUNKS, DEG_CHUNKS)].rearrange("p c j -> p (c j)")
                        nc.vector.tensor_tensor(
                            out=hot_b[:, slot], in0=tiles.unsqueeze(1).to_broadcast([P, WINDOW, DEG_CHUNKS * TILES]),
                            in1=iota_t[:, :, :], op=ALU.is_equal).then_inc(hot_b_ready, 1)

                def add_degrees(i, half):
                    firsts = first_windows(dve, i)
                    for s in range(2):
                        slot = 2 * half + s
                        dve.wait_ge(deg_product, v * 2 * STEPS + i * 2 + (s + 1 + DEG_SLOTS))
                        dve.wait_ge(deg_added, v * CHUNKS + i * UNROLL + (s + DEG_SLOTS) * DEG_CHUNKS)
                        for k in range(DEG_CHUNKS):
                            u = s * DEG_CHUNKS + k
                            to = deg_sum[32 * k:32 * k + 4, bass.ds(window_at(firsts[u], v), WINDOW)]
                            nc.vector.tensor_tensor(out=to, in0=to, in1=deg_ps[slot][32 * k:32 * k + 4, 0:WINDOW],
                                                    op=ALU.add).then_inc(deg_added, 1)

                one_hots(0, 0)
                with dve.Fori(0, STEPS // 2) as i2:
                    one_hots(i2 * 2 + 1, 1)
                    add_degrees(i2 * 2, 0)
                    one_hots(i2 * 2 + 2, 0)
                    add_degrees(i2 * 2 + 1, 1)
                add_degrees(STEPS - 1, 0)
            dve.wait_ge(deg_added, n_pass * CHUNKS + DEG_SLOTS * DEG_CHUNKS)
            dve.sem_inc(deg_summed, 1)
            link(nc.vector.memset(xT[D:D + 1, :], 1.0))
            dve.wait_ge(deg_turned, 16 * 8)
            high, mid, low, count = (deg_node[:, k::4, :] for k in range(4))
            for to, of in ((high, mid), (high, low)):
                link(nc.vector.tensor_tensor(out=to, in0=to, in1=of, op=ALU.add))
            for k, of in enumerate((deg_node[:, 0::4], deg_node[:, 3::4])):
                last = nc.vector.tensor_tensor(out=deg_max[:, :, k], in0=of[:, 0], in1=of[:, 1], op=ALU.add)
            link(last)
            nc.vector.tensor_scalar(deg_max[:], deg_max[:], 1.0, None, ALU.max).then_inc(root_in, 1)
            dve.wait_ge(root_in, 1)
            link(nc.vector.reciprocal(inv_count[:], deg_max[:, :, 1]))
            dve.wait_ge(root_out, 1)
            link(nc.vector.reciprocal(inv_root[:], deg_root[:]))
            dve.wait_ge(x_loaded, X_LOADED)
            nc.vector.tensor_copy(table_sb[:, :, D:D + 1], inv_root[:, :].unsqueeze(2)).then_inc(table_ready, 1)

            dve.wait_ge(small_loaded, 16 * 21)
            dve.wait_ge(zeroed, 4)
            GCN, SAGE_S, SAGE_N, GIN, GC1, GC2, EDGE = range(7)
            lo, hi = slice(0, D), slice(D, P)

            def scaled(to, of, by):
                return nc.vector.tensor_scalar(to, of, by, None, ALU.mult)

            def plus(to, of, by):
                return nc.vector.scalar_tensor_tensor(out=to, in0=of, scalar=by, in1=to, op0=ALU.mult, op1=ALU.add)

            link(nc.vector.tensor_scalar(gin_scale[:], eps_sb[:], 1.0, mix_sb[:, 2:3], ALU.add, ALU.mult))
            scaled(W_pair[lo, 0, 0], W_in[lo, EDGE], mix_sb[lo, 4:5])
            scaled(W_pair[hi, 0, 1], W_in[hi, GCN], mix_sb[hi, 0:1])
            scaled(W_pair[hi, 1, 1], W_in[hi, SAGE_N], mix_sb[hi, 1:2])
            scaled(W_pair[lo, 1, 0], W_in[lo, GIN], mix_sb[lo, 2:3])
            nc.vector.tensor_scalar(W_node[lo], W_in[lo, SAGE_S], mix_sb[lo, 1:2], None, ALU.mult)
            link(scaled(W_node[D:D + 1], b_in[D:D + 1, 0], mix_sb[D:D + 1, 0:1]))
            plus(W_pair[lo, 1, 0], W_in[lo, GC2], mix_sb[lo, 3:4])
            plus(W_node[lo], W_in[lo, GIN], gin_scale[lo])
            link(plus(W_node[D:D + 1], b_in[D:D + 1, 1], mix_sb[D:D + 1, 1:2]))
            plus(W_node[lo], W_in[lo, GC1], mix_sb[lo, 3:4])
            link(plus(W_node[D:D + 1], b_in[D:D + 1, 2], mix_sb[D:D + 1, 2:3]))
            nc.vector.tensor_tensor(out=W_node[lo], in0=W_node[lo], in1=ident[lo, 0:D], op=ALU.add)
            link(plus(W_node[D:D + 1], b_in[D:D + 1, 3], mix_sb[D:D + 1, 3:4]))
            link(plus(W_node[D:D + 1], b_in[D:D + 1, 4], mix_sb[D:D + 1, 4:5]))
            dve.sem_inc(weights_mixed, 1)

            link(nc.vector.memset(win_off[:], 0.0))
            with dve.Fori(0, n_pass) as v:
                window(v, n_pass * 3)
                with dve.Fori(0, STEPS) as i:
                    firsts = first_windows(dve, i)

                    def features(u):
                        c = i * UNROLL + u
                        it = v * CHUNKS + c
                        turn = v * STEPS + i + 1
                        w = e_w[:, c].unsqueeze(2).to_broadcast([P, TILES, D])
                        dve.wait_ge(chunk_product, it + 1)
                        nc.vector.tensor_tensor(
                            out=hot[:, u], in0=e_win[:, c].unsqueeze(2).to_broadcast([P, TILES, WINDOW]),
                            in1=iota_b[:, :].unsqueeze(1).to_broadcast([P, TILES, WINDOW]), op=ALU.is_equal)
                        dve.wait_ge(gathered[u], turn * (16 * TILES))
                        xs = feat[:, u, :, 3 * D:4 * D]
                        nc.vector.tensor_tensor(out=wroot[:, u], in0=e_w[:, c], in1=feat[:, u, :, 4 * D],
                                                op=ALU.mult).then_inc(wroot_ready, 1)
                        dve.wait_ge(attr_loaded[u], turn * 16)
                        nc.vector.tensor_tensor(out=attr[:, u], in0=attr[:, u], in1=xs, op=ALU.add).then_inc(summed_in, 1)
                        nc.vector.tensor_tensor(out=feat[:, u, :, 2 * D:3 * D], in0=xs, in1=w, op=ALU.mult)
                        dve.wait_ge(wroot_ready, it + 1)
                        nc.vector.tensor_tensor(out=feat[:, u, :, D:2 * D], in0=xs,
                                                in1=wroot[:, u].unsqueeze(2).to_broadcast([P, TILES, D]), op=ALU.mult)
                        dve.wait_ge(summed_in, it + 1)
                        nc.vector.scalar_tensor_tensor(out=feat[:, u, :, 0:D], in0=attr[:, u], scalar=0.0, in1=w,
                                                       op0=ALU.max, op1=ALU.mult).then_inc(feat_ready, 1)

                    def add(u):
                        c = i * UNROLL + u
                        it = v * CHUNKS + c
                        to = sums[:, :, bass.ds(window_at(firsts[u], v), WINDOW)]
                        dve.wait_ge(chunk_product, it + 1 + UNROLL)
                        dve.wait_ge(added, it + 2)
                        nc.vector.tensor_tensor(out=to, in0=to, in1=acc_ps[u % 2][:, 0:2 * WINDOW].rearrange(
                            "p (k n) -> p k n", k=2), op=ALU.add).then_inc(added, 1)

                    for u in range(UNROLL):
                        features(u)
                        if u:
                            add(u - 1)
                    add(UNROLL - 1)

            def per_node(t, tiles):
                return t[:, tiles].unsqueeze(2).to_broadcast([P, GROUP, D])

            for g in range(GROUPS):
                tiles, s = slice(g * GROUP, (g + 1) * GROUP), g % 2
                relu_gcn, wx_sage = (pair_ps[:, s, k, 0:GROUP] for k in range(2))
                t0, t1 = h_tmp[:, 2 * s], h_tmp[:, 2 * s + 1]
                dve.wait_ge(out_product, g + 1)
                nc.vector.tensor_tensor(out=t0, in0=relu_gcn[:, :, D:2 * D], in1=per_node(inv_root, tiles), op=ALU.mult)
                nc.vector.tensor_tensor(out=t1, in0=wx_sage[:, :, D:2 * D], in1=per_node(inv_count, tiles), op=ALU.mult)
                link(nc.vector.tensor_tensor(out=h[:, tiles], in0=relu_gcn[:, :, 0:D], in1=h_node[:, tiles], op=ALU.add))
                link(nc.vector.tensor_tensor(out=t0, in0=t0, in1=t1, op=ALU.add))
                nc.vector.tensor_tensor(out=h[:, tiles], in0=wx_sage[:, :, 0:D], in1=h[:, tiles], op=ALU.add).then_inc(out_taken, 1)
                dve.wait_ge(out_taken, g + 1)
                link(nc.vector.tensor_tensor(out=h[:, tiles], in0=h[:, tiles], in1=t0, op=ALU.add))
                link(nc.vector.tensor_reduce(out=mean[:, tiles], in_=h[:, tiles], axis=AX.X, op=ALU.add))
                link(nc.vector.tensor_scalar(mean[:, tiles], mean[:, tiles], 1.0 / D, None, ALU.mult))
                nc.vector.tensor_tensor(out=h[:, tiles], in0=h[:, tiles], in1=per_node(mean, tiles), op=ALU.subtract).then_inc(centred, 1)
                dve.wait_ge(squared, g + 1)
                nc.vector.tensor_reduce(out=var[:, tiles], in_=squares[:, s], axis=AX.X, op=ALU.add).then_inc(var_ready, 1)
                dve.wait_ge(root_ready, g + 1)
                link(nc.vector.reciprocal(var[:, tiles], deg_root[:, tiles]))
                nc.vector.tensor_tensor(out=h[:, tiles], in0=h[:, tiles], in1=per_node(var, tiles), op=ALU.mult).then_inc(out_ready, 1)

        @block.tensor
        def _(pe):
            pe.sem_inc(chunk_product, UNROLL)
            pe.wait_ge(consts, 4)
            pe.wait_ge(unfit_ready, 1)
            nc.tensor.matmul(misc_ps[:, 0:1], ones[:], unfit_any[:], start=True, stop=True).then_inc(unfit_counted, 1)
            pe.wait_ge(base_ready, 1)
            for g, n in groups:
                last = nc.tensor.transpose(misc_ps[0:1, P + g * P:P + g * P + n], base[0:n, g:g + 1], ident[0:n, 0:n])
            last.then_inc(base_flipped, 1)
            q = 0
            for k, rows in enumerate((row_dst, row_w, row_src)):
                if k == 1:
                    pe.wait_ge(w_loaded, ROWS_LOADED)
                for g, n in groups:
                    if k == 2:
                        pe.wait_ge(rows_ready, g + 1)
                    v = rows[:, g].rearrange("c (p j) -> c j p", j=TILES)
                    for half in range(TILES // 4):
                        q += 1
                        if 2 < q <= DST_FLIPS + 2:
                            pe.wait_ge(dst_flip_used, q - 2)
                        elif q > DST_FLIPS + 2:
                            pe.wait_ge(flip_used, q - 2 - DST_FLIPS)
                        for j in range(4):
                            last = nc.tensor.transpose(flip_ps[(q - 1) % 2][:, j * P:j * P + n],
                                                       v[0:n, 4 * half + j], ident[0:n, 0:n])
                        last.then_inc(flipped, 1)
            pe.wait_ge(base_stored, 1)
            n_pass = pe.value_load(passes[0:1, 0:1], min_val=1, max_val=WINDOWS)
            pe.sem_inc(deg_product, DEG_SLOTS)
            with pe.Fori(0, n_pass) as v:
                def sum_degrees(i, half):
                    for s in range(2):
                        slot, step = 2 * half + s, v * 2 * STEPS + i * 2 + s
                        pe.wait_ge(hot_b_ready, step + 1)
                        pe.wait_ge(w_staged, step + 1)
                        pe.wait_ge(deg_added, (step + 1) * DEG_CHUNKS)
                        for k in range(DEG_CHUNKS):
                            for j in range(TILES):
                                last = nc.tensor.matmul(deg_ps[slot][32 * k:32 * k + 4, 0:WINDOW], w_stage[:, slot, k, j],
                                                        hot_b[:, slot, :, k * TILES + j], start=(j == 0), stop=(j == TILES - 1))
                        last.then_inc(deg_product, 1)

                with pe.Fori(0, STEPS // 2) as i2:
                    sum_degrees(i2 * 2, 0)
                    sum_degrees(i2 * 2 + 1, 1)
                sum_degrees(STEPS - 1, 0)
            pe.wait_ge(deg_turned, 16 * 8)
            pe.wait_ge(x_loaded, X_LOADED)
            pe.wait_ge(flip_used, FLIPS - DST_FLIPS)
            for q in range(XFLIPS):
                if q >= 2:
                    pe.wait_ge(x_flip_used, q - 1)
                for t in range(4 * q, min(4 * q + 4, NT)):
                    last = nc.tensor.transpose(flip_ps[q % 2][0:D, (t % 4) * P:(t % 4 + 1) * P], table_sb[:, t, 0:D], ident[:])
                last.then_inc(x_flipped, 1)
            pe.wait_ge(weights_mixed, 1)
            pe.wait_ge(x_flip_used, XFLIPS)
            for g in range(GROUPS):
                if g >= 2:
                    pe.wait_ge(node_taken, g - 1)
                for n in range(GROUP):
                    t = g * GROUP + n
                    last = nc.tensor.matmul(node_ps[g % 2][:, n * D:(n + 1) * D], xT[:, t * P:(t + 1) * P], W_node[:, :],
                                            start=True, stop=True)
                last.then_inc(node_product, 1)
            with pe.Fori(0, n_pass) as v:
                with pe.Fori(0, STEPS) as i:
                    for u in range(UNROLL):
                        it = v * CHUNKS + i * UNROLL + u
                        pe.wait_ge(feat_ready, it + 1 + UNROLL)
                        pe.wait_ge(added, it + 1)
                        for k in range(2):
                            for j in range(TILES):
                                last = nc.tensor.matmul(acc_ps[u % 2][:, k * WINDOW:(k + 1) * WINDOW],
                                                        feat[:, u, j, 2 * D * k:2 * D * (k + 1)], hot[:, u, j],
                                                        start=(j == 0), stop=(j == TILES - 1))
                        last.then_inc(chunk_product, 1)
            pe.wait_ge(added, n_pass * CHUNKS + 2)
            pe.wait_ge(node_taken, GROUPS)
            for g in range(GROUPS):
                if g >= 2:
                    pe.wait_ge(out_taken, g - 1)
                for k in range(2):
                    for n in range(GROUP):
                        t = g * GROUP + n
                        last = nc.tensor.matmul(pair_ps[:, g % 2, k, n], sums[:, k, t:t + (P - 1) * NT + 1:NT],
                                                W_pair[:, k].rearrange("p a d -> p (a d)"), start=True, stop=True)
                last.then_inc(out_product, 1)


INPUTS = ("x", "src", "dst", "edge_attr_64", "edge_weight", "L0_gnn_weights", "L0_gnn_Wgcn", "L0_gnn_bgcn",
          "L0_gnn_Wsage_s", "L0_gnn_Wsage_n", "L0_gnn_bsage", "L0_gnn_gin_eps", "L0_gnn_Wgin", "L0_gnn_bgin",
          "L0_gnn_Wgc1", "L0_gnn_Wgc2", "L0_gnn_bgc", "L0_gnn_Wedge", "L0_gnn_bedge")


def kernel(**inputs):
    import concourse.bacc as bacc
    from concourse.bass_utils import run_bass_kernel_spmd

    nc = bacc.Bacc("TRN2", target_bir_lowering=False, num_devices=1)
    arrays, args = {}, []
    for name in INPUTS:
        a = np.ascontiguousarray(inputs[name])
        if a.ndim == 0 or name.endswith("gin_eps"):
            a = a.reshape(1, 1)
        arrays[f"in_{name}"] = a
        args.append(nc.dram_tensor(f"in_{name}", a.shape, mybir.dt.from_np(a.dtype), kind="ExternalInput").ap())
    out = nc.dram_tensor("out", (N, D), F32, kind="ExternalOutput").ap()
    build(nc, *args, out)
    return run_bass_kernel_spmd(nc, [arrays], core_ids=[0]).results[0]["out"]
```

```python
from contextlib import ExitStack

import concourse.bass as bass
import numpy as np
from concourse import mybir

F32 = mybir.dt.float32
BF16 = mybir.dt.bfloat16
I32 = mybir.dt.int32
U32 = mybir.dt.uint32
ALU = mybir.AluOpType
ACT = mybir.ActivationFunctionType
AX = mybir.AxisListType

P = 128
N, D = 6250, 64
E = 200000
TILES = 8
CHUNK = P * TILES
CHUNKS = -(-E // CHUNK)
LAST_START = E - CHUNK
LAST_OLD = (CHUNKS - 1) * CHUNK - LAST_START
UNROLL = 4
STEPS = CHUNKS // UNROLL
EARLY = 16
LATE = CHUNKS - EARLY
LATE_STEPS = LATE // UNROLL
WINDOW = 48
WINDOWS = -(-N // WINDOW)
NT = -(-N // P)
NPAD = P * NT
SUMS = NPAD + WINDOW
TROW = D + 4
BLOCK = D + TROW
DEG_CHUNKS = 2
DEG_SLOTS = 4
FAR = 1.0e6
EPS = 1e-5
GROUP = 7
assert CHUNKS == STEPS * UNROLL and EARLY % UNROLL == 0 and EARLY <= LATE_STEPS and NT >= WINDOW and NT % GROUP == 0 and UNROLL == 2 * DEG_CHUNKS


def build(nc, x, src, dst, edge_attr, edge_weight, mix, Wgcn, bgcn, Wsage_s, Wsage_n, bsage,
          gin_eps, Wgin, bgin, Wgc1, Wgc2, bgc, Wedge, bedge, out):
    ctx = ExitStack()
    with ctx:
        def sb(name, shape, dt=F32):
            return ctx.enter_context(nc.sbuf_tensor(name, shape, dt))

        def pb(name, shape):
            return ctx.enter_context(nc.psum_tensor(name, shape, F32))

        def sem(name):
            return ctx.enter_context(nc.semaphore(name))

        table = nc.dram_tensor("node_table", [NPAD, TROW], F32, kind="Internal").ap()

        LOW, HIGH = P, CHUNKS - P
        groups = ((0, P), (1, HIGH))
        sums = sb("sums", [P, 2, SUMS])
        area = sums[:, 0]
        raw_src, raw_dst = (area[:, k * 2 * CHUNK:(k + 1) * 2 * CHUNK].bitcast(I32).rearrange("p (g e) -> p g e", g=2)
                            for k in range(2))
        row_src = area[:, 0:2 * CHUNK].rearrange("p (g e) -> p g e", g=2)
        row_w = area[:, 4 * CHUNK:6 * CHUNK].rearrange("p (g e) -> p g e", g=2)
        attr = sb("attr", [P, UNROLL, TILES, D])
        FEATS, HOTS = UNROLL * TILES * BLOCK, UNROLL * TILES * 3 * WINDOW
        ring = sb("ring", [P, FEATS + HOTS])
        feat = ring[:, 0:FEATS].rearrange("p (u j b) -> p u j b", u=UNROLL, b=BLOCK)
        hot = ring[:, FEATS:FEATS + HOTS].rearrange("p (u j k n) -> p u j k n", u=UNROLL, k=3, n=WINDOW)
        attr_flat = attr[:, :, :, :].rearrange("p u j b -> p (u j b)")
        row_far = ring[:, SUMS + 12 * D:SUMS + 12 * D + CHUNK]
        row_dst = attr_flat[:, 0:2 * CHUNK].rearrange("p (g e) -> p g e", g=2)
        least = sb("least", [P, 2])
        most = sb("most", [P, 2])
        unfit = sb("unfit", [P, 2])
        unfit_any = sb("unfit_any", [P, 1])
        fits = sb("fits", [P, 1])
        base = sb("base", [P, 2])
        base_row = sb("base_row", [1, CHUNKS], I32)
        passes = sb("passes", [1, 1], I32)
        e_src = sb("e_src", [P, CHUNKS + UNROLL, TILES], U32)
        e_dst = sb("e_dst", [P, CHUNKS, TILES])
        e_win = sb("e_win", [P, CHUNKS, TILES], BF16)
        scratch = sb("scratch", [P, CHUNKS * TILES])
        e_tmp = scratch[:, :].rearrange("p (c j) -> p c j", j=TILES)
        e_w = sb("e_w", [P, CHUNKS, TILES])
        assert NT * D * 2 == CHUNKS * TILES * 4
        parts_h = sb("parts_h", [P, NT * D])
        w_parts = parts_h[:, :].bitcast(BF16).rearrange("p (c j k) -> p c j k", j=TILES, k=4)
        ident = sb("ident", [P, P])
        ones = sb("ones", [P, P])
        iota_b = sb("iota_b", [P, NT], BF16)
        minus_mid = sb("minus_mid", [P, 1])
        iota_t = sb("iota_t", [P, WINDOW, DEG_CHUNKS * TILES], BF16)
        win_off = sb("win_off", [P, 1])
        w_stage = sb("w_stage", [P, DEG_SLOTS, DEG_CHUNKS, TILES, 4], BF16)
        hot_b = scratch[:, :].bitcast(BF16)[:, 0:DEG_SLOTS * WINDOW * DEG_CHUNKS * TILES].rearrange(
            "p (s n j) -> p s n j", s=DEG_SLOTS, n=WINDOW)
        deg_sum = ring[:, 0:SUMS]
        deg_node = scratch[:, 0:2 * 4 * NT].rearrange("p (k t) -> p k t", t=NT)
        deg_max = sb("deg_max", [P, NT, 2])
        deg_root = sb("deg_root", [P, NT])
        root_part = sb("root_part", [P, NT + 1])
        inv_root = root_part[:, 0:NT]
        inv_count = sb("inv_count", [P, NT])
        table_sb = sb("table_sb", [P, NT, TROW])
        idx = sb("idx", [P, UNROLL, TILES], U32)
        wroot = sb("wroot", [P, UNROLL, TILES])
        early_idx = sb("early_idx", [P, EARLY, TILES], U32)
        early_x = sb("early_x", [P, EARLY, TILES, D])
        wroot_e = sb("wroot_e", [P, TILES])
        root_src = sb("root_src", [P, TILES])
        low_src = sb("low_src", [P, TILES])
        sizes = (2 * TILES * D, TILES * D, TILES * 3 * WINDOW, CHUNK, TILES * NT, TILES * NT)
        ends = np.cumsum(sizes).tolist()
        early = sb("early", [P, ends[-1]])
        feat_e, attr_e, hot_e, high_e, low_e, picked = (early[:, b - n:b] for b, n in zip(ends, sizes))
        feat_e, attr_e, low_e, picked = (t.rearrange("p (j n) -> p j n", j=TILES) for t in (feat_e, attr_e, low_e, picked))
        hot_e = hot_e.rearrange("p (j k n) -> p j k n", j=TILES, k=3)
        src_all = high_e.bitcast(I32)
        xT = early[0:D + 1, 0:2 * GROUP * P].rearrange("p (s c) -> p s c", s=2)
        W_in = ring[:, SUMS:SUMS + 7 * D].rearrange("p (k d) -> p k d", d=D)
        b_in = ring[0:D + 1, SUMS + 7 * D:SUMS + 12 * D].rearrange("p (k d) -> p k d", d=D)
        mix_sb = sb("mix_sb", [P, 5])
        eps_sb = sb("eps_sb", [P, 1])
        eps_ln = sb("eps_ln", [P, 1])
        gin_scale = sb("gin_scale", [P, 1])
        W_node = sb("W_node", [D + 1, D])
        W_sum = sb("W_sum", [P, D])
        W_pair = sb("W_pair", [P, 2, D])
        h_node = parts_h[:, :].rearrange("p (t d) -> p t d", d=D)
        h = ring[:, 0:NT * D].rearrange("p (t d) -> p t d", d=D)
        h_tmp = ring[:, NT * D:(NT + 4 * GROUP) * D].rearrange("p (k t d) -> p k t d", k=4, d=D)
        squares = attr_flat[:, 0:2 * GROUP * D].rearrange("p (s t d) -> p s t d", s=2, d=D)
        mean = sb("mean", [P, NT])
        var = sb("var", [P, NT])

        psum = pb("psum", [P, 8 * 512])
        bank = [psum[:, k * 512:(k + 1) * 512] for k in range(8)]
        acc_ps, flip_ps, misc_ps, node_ps, deg_ps = bank[0:2], bank[2:4], bank[4], bank[5:7], bank[0:2] + bank[5:7]
        acc_e, root_ps = bank[7], bank[4]
        x_ps = [psum[0:D, s * 1024:s * 1024 + GROUP * P] for s in range(2)]
        sum_ps = [psum[:, s * 2048:s * 2048 + GROUP * D].rearrange("p (t c) -> p t c", c=D) for s in range(2)]
        pair_ps = [psum[:, s * 2048 + 512:s * 2048 + 512 + GROUP * 2 * D].rearrange("p (t c) -> p t c", c=2 * D)
                   for s in range(2)]

        dst_loaded, src_loaded, w_loaded = sem("dst_loaded"), sem("src_loaded"), sem("w_loaded")
        far_ready, pad_x, zeroed = sem("far_ready"), sem("pad_x"), sem("zeroed")
        x_loaded, small_loaded = sem("x_loaded"), sem("small_loaded")
        consts = sem("consts")
        gathers_begun, windows_set = sem("gathers_begun"), sem("windows_set")
        dve_chain, pass_step = sem("dve_chain"), sem("pass_step")
        pool_chain = sem("pool_chain")
        unfit_ready, unfit_counted = sem("unfit_ready"), sem("unfit_counted")
        base_ready, base_flipped, base_stored = sem("base_ready"), sem("base_flipped"), sem("base_stored")
        rows_ready, flipped, flip_used = sem("rows_ready"), sem("flipped"), sem("flip_used")
        dst_flip_used = sem("dst_flip_used")
        w_high, w_split = sem("w_high"), sem("w_split")
        w_staged, src_wrapped = sem("w_staged"), sem("src_wrapped")
        deg_summed, deg_turned = sem("deg_summed"), sem("deg_turned")
        hot_b_ready, deg_product, deg_added = sem("hot_b_ready"), sem("deg_product"), sem("deg_added")
        root_in, root_out = sem("root_in"), sem("root_out")
        table_ready, table_stored = sem("table_ready"), sem("table_stored")
        x_flipped, x_flip_used, ones_row = sem("x_flipped"), sem("x_flip_used"), sem("ones_row")
        node_product, node_taken = sem("node_product"), sem("node_taken")
        staged = sem("staged")
        gathered = [sem(f"gathered{u}") for u in range(UNROLL)]
        attr_loaded = [sem(f"attr_loaded{u}") for u in range(UNROLL)]
        hot_made, wroot_ready, hots_ready = sem("hot_made"), sem("wroot_ready"), sem("hots_ready")
        summed_in = sem("summed_in")
        relu_ready = sem("relu_ready")
        chunk_product = sem("chunk_product")
        early_idx_loaded, early_gathered = sem("early_idx_loaded"), sem("early_gathered")
        src_all_loaded, attr_e_loaded = sem("src_all_loaded"), sem("attr_e_loaded")
        distance_ready, high_ready, low_ready = sem("distance_ready"), sem("high_ready"), sem("low_ready")
        roots_product, early_chain, early_copied = sem("roots_product"), sem("early_chain"), sem("early_copied")
        early_summed, early_hots_ready = sem("early_summed"), sem("early_hots_ready")
        early_relu_ready, early_product, early_added = sem("early_relu_ready"), sem("early_product"), sem("early_added")
        added = sem("added")
        weights_mixed = sem("weights_mixed")
        out_product, out_taken = sem("out_product"), sem("out_taken")
        centred, squared, var_ready, root_ready = sem("centred"), sem("squared"), sem("var_ready"), sem("root_ready")
        out_ready, stored = sem("out_ready"), sem("stored")

        FLIPS = 3 * 2 * (TILES // 4)
        DST_FLIPS = FLIPS // 3
        GROUPS = NT // GROUP

        block = ctx.enter_context(nc.Block())

        flat_w, flat_tmp = e_w[:, :, :].rearrange("p c j -> p (c j)"), scratch[:, :]
        parts = w_parts[:, :, :, :].rearrange("p c j k -> p (c j) k")

        def flip_place(t, g, n, half):
            return t[:, g * P:g * P + n, 4 * half:4 * half + 4].rearrange("p c j -> p j c")

        def flip_of(q, n):
            return flip_ps[(q - 1) % 2].rearrange("p (j c) -> p j c", j=4)[:, :, 0:n]

        def first_windows(eng, c, n):
            return nc.values_load_multi_w_load_instructions(
                base_row[0:1, bass.ds(c, n)], engines=(eng.engine,), min_val=0, max_val=N - 1,
                skip_runtime_bounds_check_because="destinations are nodes")[1]

        def window_at(first, v):
            return nc.s_assert_within(first + v * WINDOW, 0, NPAD,
                                      skip_runtime_bounds_check_because="first is 0 in all passes but the first")

        def rows_of(t, c0, c1):
            return t[c0 * CHUNK:c1 * CHUNK].rearrange("(c e) -> c e", e=CHUNK)

        def load_rows(eng, t, rows, loaded):
            eng.dma_start(rows[:, 0, :], rows_of(t, 0, P)).then_inc(loaded, 16)
            full = CHUNKS - 1 - P
            cut = full - full % 16
            eng.dma_start(rows[0:cut, 1, :], rows_of(t, P, P + cut)).then_inc(loaded, 16)
            eng.dma_start(rows[cut:full, 1, :], rows_of(t, P + cut, P + full)).then_inc(loaded, 16)
            eng.dma_start(rows[full:full + 1, 1, :],
                          t[LAST_START:E].rearrange("(a e) -> a e", a=1)).then_inc(loaded, 16)

        ROWS_LOADED = 4 * 16

        def node_rows(t, rows):
            full = N // NT
            cut = full - full % 16
            v = t[0:full * NT, :].rearrange("(p t) d -> p t d", t=NT)
            rest = N - full * NT
            return ((v[0:cut], rows[0:cut]), (v[cut:full], rows[cut:full]),
                    (t[full * NT:N, :].rearrange("(p t) d -> p t d", p=1), rows[full:full + 1, 0:rest]))

        X_LOADED = 3 * 16

        @block.sync
        def _(sp):
            sp.dma_start(early_idx[:, :, :].bitcast(I32), src[0:EARLY * CHUNK].rearrange(
                "(c p j) -> p c j", p=P, j=TILES)).then_inc(early_idx_loaded, 16)
            load_rows(sp, dst, raw_dst, dst_loaded)
            load_rows(sp, src, raw_src, src_loaded)
            sp.wait_ge(pad_x, 1)
            for of, to in node_rows(x, table_sb[:, :, 0:D]):
                sp.dma_start(to, of).then_inc(x_loaded, 16)
            sp.wait_ge(deg_summed, 1)
            for k in range(DEG_CHUNKS):
                for part in range(4):
                    row = 32 * k + part
                    sp.dma_start(deg_node[:, 4 * k + part, :],
                                 deg_sum[row:row + 1, 0:NPAD].rearrange("k (p t) -> k p t", t=NT)).then_inc(deg_turned, 16)
            sp.wait_ge(table_ready, 1)
            sp.dma_start(table.rearrange("(p t) d -> p (t d)", p=P),
                         table_sb[:, :, :].rearrange("p t d -> p (t d)")).then_inc(table_stored, 16)
            sp.wait_ge(base_stored, 1)
            n_pass = sp.value_load(passes[0:1, 0:1], min_val=1, max_val=WINDOWS)
            with sp.Fori(0, n_pass) as v:
                def load_attributes(i, u):
                    start = (i * UNROLL + u + EARLY) * CHUNK
                    if u == UNROLL - 1:
                        start = nc.s_assert_within(
                            start - (i // (LATE_STEPS - 1)) * ((CHUNKS - 1) * CHUNK - LAST_START), min_val=0,
                            max_val=LAST_START, skip_runtime_bounds_check_because="the last chunk is moved back")
                    sp.wait_ge(relu_ready, v * LATE + i * UNROLL + u + 1)
                    sp.dma_start(attr[:, u, :, :].rearrange("p j d -> p (j d)"),
                                 edge_attr[bass.ds(start, CHUNK), :].rearrange(
                                     "(p j) d -> p (j d)", p=P)).then_inc(attr_loaded[u], 16)

                with sp.Fori(0, EARLY) as i:
                    for u in range(UNROLL):
                        load_attributes(i, u)
                        if u == 1:
                            sp.wait_ge(node_taken, GROUPS)
                            sp.wait_ge(roots_product, v * EARLY + i + 1)
                            sp.dma_start(src_all, src[bass.ds(i * CHUNK, CHUNK)].rearrange("(a e) -> a e", a=1)
                                         .to_broadcast([P, CHUNK])).then_inc(src_all_loaded, 16)
                            sp.wait_ge(early_relu_ready, v * EARLY + i + 1)
                            sp.dma_start(attr_e.rearrange("p j d -> p (j d)"),
                                         edge_attr[bass.ds(i * CHUNK, CHUNK), :].rearrange(
                                             "(p j) d -> p (j d)", p=P)).then_inc(attr_e_loaded, 16)
                with sp.Fori(EARLY, LATE_STEPS) as i:
                    for u in range(UNROLL):
                        load_attributes(i, u)
            full, rest = N // NT, N % NT
            cut, n_out = full - full % 16, 0
            of_full = out[0:full * NT, :].rearrange("(p t) d -> p t d", t=NT)
            of_last = out[full * NT:N, :].rearrange("(p t) d -> p t d", p=1)
            for g in range(GROUPS):
                sp.wait_ge(out_ready, g + 1)
                t0, t1 = g * GROUP, (g + 1) * GROUP
                for p0, p1 in ((0, cut), (cut, full)):
                    sp.dma_start(of_full[p0:p1, t0:t1], h[p0:p1, t0:t1]).then_inc(stored, 16)
                    n_out += 1
                if t0 < rest:
                    sp.dma_start(of_last[:, t0:min(t1, rest)], h[full:full + 1, t0:min(t1, rest)]).then_inc(stored, 16)
                    n_out += 1
            sp.wait_ge(stored, 16 * n_out)

        @block.gpsimd
        def _(pool):
            nc.gpsimd.memset(ident[:], 0.0).then_inc(pool_chain, 1)
            nc.gpsimd.memset(row_far[:], 0.0).then_inc(pool_chain, 1)
            nc.gpsimd.memset(ones[:], 1.0).then_inc(consts, 1)
            pool.wait_ge(pool_chain, 2)
            nc.gpsimd.affine_select(out=ident[:], in_=ident[:], compare_op=ALU.not_equal, fill=1.0, base=0,
                                    pattern=[[-1, P]], channel_multiplier=1).then_inc(consts, 1)
            nc.gpsimd.affine_select(out=row_far[:, 0:LAST_OLD], in_=row_far[:, 0:LAST_OLD], compare_op=ALU.not_equal,
                                    fill=FAR, base=-(HIGH - 1), pattern=[[0, LAST_OLD]],
                                    channel_multiplier=1).then_inc(far_ready, 1)
            nc.gpsimd.iota(iota_b[:], [[1, NT]], base=0, channel_multiplier=0,
                           allow_small_or_imprecise_dtypes=True).then_inc(consts, 1)
            nc.gpsimd.iota(iota_t[:], [[1, WINDOW], [0, DEG_CHUNKS * TILES]], base=0, channel_multiplier=0,
                           allow_small_or_imprecise_dtypes=True).then_inc(consts, 1)
            nc.gpsimd.memset(w_parts[:, :, :, 3:4], 1.0).then_inc(zeroed, 1)
            nc.gpsimd.memset(deg_sum[:], 0.0).then_inc(zeroed, 1)
            pool.wait_ge(early_idx_loaded, 16)
            for c in range(EARLY):
                for j in range(TILES):
                    nc.gpsimd.indirect_dma_start(
                        out=early_x[:, c, j], out_offset=None, in_=x,
                        in_offset=bass.IndirectOffsetOnAxis(ap=early_idx[:, c, j:j + 1], axis=0),
                    ).then_inc(early_gathered, 16)
                if c == 0:
                    nc.gpsimd.iota(root_part[:, NT:NT + 1], [[0, 1]], base=0, channel_multiplier=1,
                                   allow_small_or_imprecise_dtypes=True).then_inc(consts, 1)
                    nc.gpsimd.iota(minus_mid[:], [[0, 1]], base=-(NT // 2), channel_multiplier=-NT,
                                   allow_small_or_imprecise_dtypes=True).then_inc(consts, 1)
                    nc.gpsimd.memset(table_sb[:], 0.0).then_inc(pad_x, 1)
                    nc.gpsimd.memset(W_pair[:], 0.0).then_inc(zeroed, 1)
            pool.wait_ge(flip_used, FLIPS - DST_FLIPS)
            nc.gpsimd.memset(sums[:], 0.0).then_inc(zeroed, 1)
            pool.wait_ge(table_stored, 16)
            pool.wait_ge(base_stored, 1)
            n_pass = pool.value_load(passes[0:1, 0:1], min_val=1, max_val=WINDOWS)
            with pool.Fori(0, n_pass) as v:
                with pool.Fori(0, LATE_STEPS) as i:
                    for u in range(UNROLL):
                        it = v * LATE + i * UNROLL + u
                        pool.wait_ge(staged, it + 1)
                        pool.wait_ge(chunk_product, it + 1)
                        pool.sem_inc(gathers_begun, 1)
                        for j in range(TILES):
                            nc.gpsimd.indirect_dma_start(
                                out=feat[:, u, j, D:BLOCK], out_offset=None, in_=table,
                                in_offset=bass.IndirectOffsetOnAxis(ap=idx[:, u, j:j + 1], axis=0),
                            ).then_inc(gathered[u], 16)

        @block.scalar
        def _(act):
            load_rows(act, edge_weight, row_w, w_loaded)
            for k, W in enumerate((Wgcn, Wsage_s, Wsage_n, Wgin, Wgc1, Wgc2, Wedge)):
                for half in range(2):
                    act.dma_start(W_in[half * D:(half + 1) * D, k, :], W).then_inc(small_loaded, 16)
            for k, b in enumerate((bgcn, bsage, bgin, bgc, bedge)):
                act.dma_start(b_in[D:D + 1, k, :], b.rearrange("(a d) -> a d", a=1)).then_inc(small_loaded, 16)
            act.dma_start(mix_sb[:, :], mix.rearrange("(a k) -> a k", a=1).to_broadcast([P, 5])).then_inc(small_loaded, 16)
            act.dma_start(eps_sb[:, :], gin_eps.to_broadcast([P, 1])).then_inc(small_loaded, 16)

            q = DST_FLIPS
            for to in (e_w, e_src):
                if to is e_src:
                    act.wait_ge(src_loaded, ROWS_LOADED)
                    for g, n in groups:
                        nc.scalar.copy(row_src[0:n, g], raw_src[0:n, g]).then_inc(rows_ready, 1)
                for g, n in groups:
                    for half in range(TILES // 4):
                        q += 1
                        act.wait_ge(flipped, q)
                        nc.scalar.copy(flip_place(to, g, n, half), flip_of(q, n)).then_inc(flip_used, 1)
                if to is e_w:
                    act.wait_ge(flip_used, q - DST_FLIPS)
                    nc.scalar.copy(parts[:, :, 0], flat_w).then_inc(w_high, 1)
            act.wait_ge(flip_used, FLIPS - DST_FLIPS)
            nc.scalar.copy(idx[:, :, :], e_src[:, EARLY:EARLY + UNROLL]).then_inc(staged, UNROLL)
            nc.scalar.copy(e_src[:, CHUNKS:CHUNKS + UNROLL], e_src[:, EARLY:EARLY + UNROLL]).then_inc(src_wrapped, 1)
            act.wait_ge(src_wrapped, 1)
            act.wait_ge(base_stored, 1)
            n_pass = act.value_load(passes[0:1, 0:1], min_val=1, max_val=WINDOWS)
            act.wait_ge(w_split, 1)
            act.wait_ge(zeroed, 1)
            with act.Fori(0, n_pass) as v:
                act.wait_ge(deg_product, v * 2 * STEPS + DEG_SLOTS)

                def stage_weights(i, half):
                    for s in range(2):
                        act.wait_ge(deg_product, v * 2 * STEPS + i * 2 + s + 1)
                        nc.scalar.copy(w_stage[:, 2 * half + s],
                                       w_parts[:, bass.ds(i * UNROLL + s * DEG_CHUNKS, DEG_CHUNKS)]).then_inc(w_staged, 1)

                with act.Fori(0, STEPS // 2) as i2:
                    stage_weights(i2 * 2, 0)
                    stage_weights(i2 * 2 + 1, 1)
                stage_weights(STEPS - 1, 0)
            act.wait_ge(root_in, 1)
            nc.scalar.activation(deg_root[:], deg_max[:, :, 0], ACT.Sqrt).then_inc(root_out, 1)
            for g in range(GROUPS + 1):
                if g < GROUPS:
                    act.wait_ge(x_flipped, g + 1)
                    if g == 0:
                        act.wait_ge(ones_row, 1)
                    nc.scalar.copy(xT[0:D, g % 2], x_ps[g % 2]).then_inc(x_flip_used, 1)
                if g > 0:
                    act.wait_ge(node_product, g)
                    nc.scalar.copy(h_node[:, (g - 1) * GROUP:g * GROUP],
                                   node_ps[(g - 1) % 2][:, 0:GROUP * D].rearrange("p (t d) -> p t d", d=D)
                                   ).then_inc(node_taken, 1)
            act.sem_inc(relu_ready, UNROLL)
            act.sem_inc(early_relu_ready, 1)
            act.wait_ge(consts, 6)
            act.wait_ge(node_taken, GROUPS)
            act.wait_ge(early_gathered, EARLY * TILES * 16)
            with act.Fori(0, n_pass) as v:
                def late_step(i, early):
                    for u in range(UNROLL):
                        act.wait_ge(gathered[u], (v * LATE_STEPS + i + 1) * (16 * TILES))
                        nc.scalar.copy(idx[:, u], e_src[:, (i + 1) * UNROLL + u + EARLY]).then_inc(staged, 1)
                        act.wait_ge(summed_in, v * LATE + i * UNROLL + u + 1)
                        nc.scalar.activation(feat[:, u, :, 0:D], attr[:, u], ACT.Relu).then_inc(relu_ready, 1)
                        if early and u == 1:
                            act.wait_ge(early_summed, v * EARLY + i + 1)
                            nc.scalar.activation(feat_e[:, :, 0:D], attr_e, ACT.Relu).then_inc(early_relu_ready, 1)

                with act.Fori(0, EARLY) as i:
                    act.wait_ge(src_all_loaded, (v * EARLY + i + 1) * 16)
                    nc.scalar.activation(high_e, src_all, ACT.Square, bias=minus_mid[:]).then_inc(distance_ready, 1)
                    act.wait_ge(early_product, v * EARLY + i + 1)
                    nc.scalar.copy(feat_e[:, :, D:2 * D], early_x[:, i]).then_inc(early_copied, 1)
                    late_step(i, True)
                with act.Fori(EARLY, LATE_STEPS) as i:
                    late_step(i, False)
            for g in range(GROUPS):
                tiles = slice(g * GROUP, (g + 1) * GROUP)
                act.wait_ge(centred, g + 1)
                nc.scalar.activation(squares[:, g % 2], h[:, tiles], ACT.Square).then_inc(squared, 1)
                act.wait_ge(var_ready, g + 1)
                nc.scalar.activation(deg_root[:, tiles], var[:, tiles], ACT.Sqrt, bias=eps_ln[:], scale=1.0 / D
                                     ).then_inc(root_ready, 1)

        @block.vector
        def _(dve):
            chain = [0]

            def link(ins):
                chain[0] += 1
                ins.then_inc(dve_chain, 1)
                dve.wait_ge(dve_chain, chain[0])

            dve.sem_inc(deg_added, DEG_SLOTS * DEG_CHUNKS)
            dve.sem_inc(added, 2 * 3)
            dve.sem_inc(early_added, 3)
            nc.vector.memset(eps_ln[:], EPS)
            nc.vector.memset(least[:], 0.0)
            link(nc.vector.memset(most[:], 0.0))
            dve.wait_ge(dst_loaded, ROWS_LOADED)
            for g, n in groups:
                nc.vector.tensor_reduce(out=least[0:n, g:g + 1], in_=raw_dst[0:n, g], axis=AX.X, op=ALU.min)
                last = nc.vector.tensor_reduce(out=most[0:n, g:g + 1], in_=raw_dst[0:n, g], axis=AX.X, op=ALU.max)
            link(last)
            link(nc.vector.tensor_tensor(out=unfit[:], in0=most[:], in1=least[:], op=ALU.subtract))
            link(nc.vector.tensor_scalar(unfit[:], unfit[:], WINDOW - 0.5, None, ALU.is_gt))
            nc.vector.tensor_reduce(out=unfit_any[:], in_=unfit[:], axis=AX.X, op=ALU.max).then_inc(unfit_ready, 1)
            dve.wait_ge(unfit_counted, 1)
            link(nc.vector.tensor_scalar(fits[:], misc_ps[:, 0:1], 0.5, None, ALU.is_lt))
            nc.vector.tensor_scalar(passes[:], fits[0:1, :], 1.0 - WINDOWS, float(WINDOWS), ALU.mult, ALU.add)
            link(nc.vector.tensor_scalar(base[:], least[:], fits[:, 0:1], None, ALU.mult))
            nc.vector.tensor_scalar(row_dst[:, 0], raw_dst[:, 0], base[:, 0:1], None, ALU.subtract)
            dve.wait_ge(far_ready, 1)
            nc.vector.scalar_tensor_tensor(out=row_dst[0:HIGH, 1], in0=raw_dst[0:HIGH, 1], scalar=base[0:HIGH, 1:2],
                                           in1=row_far[0:HIGH], op0=ALU.subtract, op1=ALU.add).then_inc(base_ready, 1)
            dve.wait_ge(base_flipped, 1)
            nc.vector.tensor_copy(base_row[:], misc_ps[0:1, P:P + CHUNKS]).then_inc(base_stored, 1)
            q = 0
            for g, n in groups:
                for half in range(TILES // 4):
                    q += 1
                    dve.wait_ge(flipped, q)
                    nc.vector.tensor_copy(flip_place(e_dst, g, n, half), flip_of(q, n)).then_inc(dst_flip_used, 1)
            dve.wait_ge(dst_flip_used, DST_FLIPS)
            dve.wait_ge(w_high, 1)
            link(nc.vector.tensor_tensor(out=flat_tmp, in0=flat_w, in1=parts[:, :, 0], op=ALU.subtract))
            link(nc.vector.tensor_copy(parts[:, :, 1], flat_tmp))
            nc.vector.tensor_tensor(out=parts[:, :, 2], in0=flat_tmp, in1=parts[:, :, 1], op=ALU.subtract).then_inc(w_split, 1)
            dve.wait_ge(w_split, 1)
            n_pass = dve.value_load(passes[0:1, 0:1], min_val=1, max_val=WINDOWS)

            def window(v, count):
                nc.vector.tensor_scalar(e_tmp[:], e_dst[:], win_off[:, 0:1], -1.0, ALU.subtract, ALU.max).then_inc(pass_step, 1)
                dve.wait_ge(pass_step, count + v * 3 + 1)
                nc.vector.tensor_scalar(e_win[:], e_tmp[:], float(WINDOW), None, ALU.min).then_inc(pass_step, 1)
                nc.vector.tensor_scalar(win_off[:], win_off[:], float(WINDOW), None, ALU.add).then_inc(pass_step, 1)
                dve.wait_ge(pass_step, count + v * 3 + 3)
                dve.sem_inc(windows_set, 1)

            dve.wait_ge(consts, 4)
            link(nc.vector.memset(win_off[:], 0.0))
            dve.wait_ge(zeroed, 2)
            with dve.Fori(0, n_pass) as v:
                window(v, 0)
                def one_hots(i, half):
                    before = dve.snap(v * 2 * STEPS + i * 2)
                    for s in range(2):
                        slot = 2 * half + s
                        dve.wait_ge(deg_product, before + (s + 1))
                        tiles = e_win[:, bass.ds(i * UNROLL + s * DEG_CHUNKS, DEG_CHUNKS)].rearrange("p c j -> p (c j)")
                        nc.vector.tensor_tensor(
                            out=hot_b[:, slot], in0=tiles.unsqueeze(1).to_broadcast([P, WINDOW, DEG_CHUNKS * TILES]),
                            in1=iota_t[:, :, :], op=ALU.is_equal).then_inc(hot_b_ready, 1)

                def add_degrees(i, half):
                    firsts = first_windows(dve, i * UNROLL, UNROLL)
                    for s in range(2):
                        slot = 2 * half + s
                        dve.wait_ge(deg_product, v * 2 * STEPS + i * 2 + (s + 1 + DEG_SLOTS))
                        dve.wait_ge(deg_added, v * CHUNKS + i * UNROLL + (s + DEG_SLOTS) * DEG_CHUNKS)
                        for k in range(DEG_CHUNKS):
                            u = s * DEG_CHUNKS + k
                            to = deg_sum[32 * k:32 * k + 4, bass.ds(window_at(firsts[u], v), WINDOW)]
                            nc.vector.tensor_tensor(out=to, in0=to, in1=deg_ps[slot][32 * k:32 * k + 4, 0:WINDOW],
                                                    op=ALU.add).then_inc(deg_added, 1)

                one_hots(0, 0)
                with dve.Fori(0, STEPS // 2) as i2:
                    one_hots(i2 * 2 + 1, 1)
                    add_degrees(i2 * 2, 0)
                    one_hots(i2 * 2 + 2, 0)
                    add_degrees(i2 * 2 + 1, 1)
                add_degrees(STEPS - 1, 0)
            dve.wait_ge(deg_added, n_pass * CHUNKS + DEG_SLOTS * DEG_CHUNKS)
            dve.sem_inc(deg_summed, 1)
            nc.vector.memset(xT[D:D + 1], 1.0).then_inc(ones_row, 1)

            dve.wait_ge(small_loaded, 16 * 21)
            dve.wait_ge(zeroed, 3)
            GCN, SAGE_S, SAGE_N, GIN, GC1, GC2, EDGE = range(7)
            lo, hi = slice(0, D), slice(D, P)

            def scaled(to, of, by):
                return nc.vector.tensor_scalar(to, of, by, None, ALU.mult)

            def plus(to, of, by):
                return nc.vector.scalar_tensor_tensor(out=to, in0=of, scalar=by, in1=to, op0=ALU.mult, op1=ALU.add)

            link(nc.vector.tensor_scalar(gin_scale[:], eps_sb[:], 1.0, mix_sb[:, 2:3], ALU.add, ALU.mult))
            scaled(W_sum[lo], W_in[lo, EDGE], mix_sb[lo, 4:5])
            scaled(W_sum[hi], W_in[hi, GIN], mix_sb[hi, 2:3])
            scaled(W_pair[lo, 0], W_in[lo, GCN], mix_sb[lo, 0:1])
            scaled(W_pair[hi, 1], W_in[hi, SAGE_N], mix_sb[hi, 1:2])
            nc.vector.tensor_scalar(W_node[lo], W_in[lo, SAGE_S], mix_sb[lo, 1:2], None, ALU.mult)
            link(scaled(W_node[D:D + 1], b_in[D:D + 1, 0], mix_sb[D:D + 1, 0:1]))
            plus(W_sum[hi], W_in[hi, GC2], mix_sb[hi, 3:4])
            plus(W_node[lo], W_in[lo, GIN], gin_scale[lo])
            link(plus(W_node[D:D + 1], b_in[D:D + 1, 1], mix_sb[D:D + 1, 1:2]))
            plus(W_node[lo], W_in[lo, GC1], mix_sb[lo, 3:4])
            link(plus(W_node[D:D + 1], b_in[D:D + 1, 2], mix_sb[D:D + 1, 2:3]))
            nc.vector.tensor_tensor(out=W_node[lo], in0=W_node[lo], in1=ident[lo, 0:D], op=ALU.add)
            link(plus(W_node[D:D + 1], b_in[D:D + 1, 3], mix_sb[D:D + 1, 3:4]))
            link(plus(W_node[D:D + 1], b_in[D:D + 1, 4], mix_sb[D:D + 1, 4:5]))
            dve.sem_inc(weights_mixed, 1)

            dve.wait_ge(deg_turned, 16 * 8)
            high, mid, low, count = (deg_node[:, k::4, :] for k in range(4))
            for to, of in ((high, mid), (high, low)):
                link(nc.vector.tensor_tensor(out=to, in0=to, in1=of, op=ALU.add))
            for k, of in enumerate((deg_node[:, 0::4], deg_node[:, 3::4])):
                last = nc.vector.tensor_tensor(out=deg_max[:, :, k], in0=of[:, 0], in1=of[:, 1], op=ALU.add)
            link(last)
            nc.vector.tensor_scalar(deg_max[:], deg_max[:], 1.0, None, ALU.max).then_inc(root_in, 1)
            dve.wait_ge(root_in, 1)
            link(nc.vector.reciprocal(inv_count[:], deg_max[:, :, 1]))
            dve.wait_ge(root_out, 1)
            link(nc.vector.reciprocal(inv_root[:], deg_root[:]))
            dve.wait_ge(x_loaded, X_LOADED)
            nc.vector.tensor_copy(table_sb[:, :, D:D + 1], inv_root[:, :].unsqueeze(2)).then_inc(table_ready, 1)

            dve.wait_ge(zeroed, 4)
            link(nc.vector.memset(win_off[:], 0.0))
            with dve.Fori(0, n_pass) as v:
                window(v, n_pass * 3)
                def late_step(i, early):
                    firsts = first_windows(dve, EARLY + i * UNROLL, UNROLL)

                    def features(u):
                        c = i * UNROLL + u + EARLY
                        it = v * LATE + i * UNROLL + u
                        turn = v * LATE_STEPS + i + 1
                        dve.wait_ge(chunk_product, it + 1)
                        window_hots(hot[:, u], c).then_inc(hot_made, 1)
                        dve.wait_ge(hot_made, it + 1)
                        weigh(hot[:, u], 1, e_w[:, c])
                        dve.wait_ge(gathered[u], turn * (16 * TILES))
                        nc.vector.tensor_tensor(out=wroot[:, u], in0=e_w[:, c], in1=feat[:, u, :, 2 * D],
                                                op=ALU.mult).then_inc(wroot_ready, 1)
                        dve.wait_ge(attr_loaded[u], turn * 16)
                        nc.vector.tensor_tensor(out=attr[:, u], in0=attr[:, u], in1=feat[:, u, :, D:2 * D],
                                                op=ALU.add).then_inc(summed_in, 1)
                        dve.wait_ge(wroot_ready, it + 1)
                        weigh(hot[:, u], 2, wroot[:, u]).then_inc(hots_ready, 1)

                    def add(u):
                        it = v * LATE + i * UNROLL + u
                        dve.wait_ge(chunk_product, it + 1 + UNROLL)
                        if u == 0:
                            dve.wait_ge(early_added, (v * EARLY + (i if early else EARLY) + 1) * 3)
                        dve.wait_ge(added, (it + 2) * 3)
                        add_sums(acc_ps[u % 2], firsts[u], added)

                    if early:
                        dve.wait_ge(distance_ready, v * EARLY + i + 1)
                        nc.vector.tensor_scalar(high_e, high_e, (NT // 2 + 0.5) ** 2, None, ALU.is_lt).then_inc(high_ready, 1)
                    for u in range(UNROLL):
                        features(u)
                        if u:
                            add(u - 1)
                        if early and u == 1:
                            early_features(i)
                    add(UNROLL - 1)
                    if early:
                        first, = first_windows(dve, i, 1)
                        dve.wait_ge(early_product, v * EARLY + i + 2)
                        dve.wait_ge(added, (v * LATE + (i + 1) * UNROLL + 2) * 3)
                        add_sums(acc_e, first, early_added)

                def add_sums(acc, first, done):
                    to = bass.ds(window_at(first, v), WINDOW)
                    for of, k, part in ((slice(0, P), 0, 1), (slice(D, P), 1, 0), (slice(0, D), 1, 2)):
                        ps = slice(D, P) if part == 2 else of
                        nc.vector.tensor_tensor(out=sums[of, k, to], in0=sums[of, k, to],
                                                in1=acc[ps, part * WINDOW:(part + 1) * WINDOW], op=ALU.add).then_inc(done, 1)

                def window_hots(to, c):
                    return nc.vector.tensor_tensor(
                        out=to[:, :, 0], in0=e_win[:, c].unsqueeze(2).to_broadcast([P, TILES, WINDOW]),
                        in1=iota_b[:, 0:WINDOW].unsqueeze(1).to_broadcast([P, TILES, WINDOW]), op=ALU.is_equal)

                def weigh(to, k, by):
                    return nc.vector.tensor_tensor(out=to[:, :, k], in0=to[:, :, 0],
                                                   in1=by.unsqueeze(2).to_broadcast([P, TILES, WINDOW]), op=ALU.mult)

                def early_features(c):
                    n = v * EARLY + c
                    count = dve.snap(n * 5)
                    steps = [0]

                    def then(ins):
                        steps[0] += 1
                        ins.then_inc(early_chain, 1)
                        dve.wait_ge(early_chain, count + steps[0])

                    by_tile = root_ps[:, 0:TILES * (NT + 1)].rearrange("p (j n) -> p j n", j=TILES)
                    dve.wait_ge(roots_product, n + 2)
                    then(nc.vector.scalar_tensor_tensor(out=low_src[:], in0=by_tile[:, :, NT], scalar=float(-NT),
                                                        in1=e_src[:, c], op0=ALU.mult, op1=ALU.add))
                    then(nc.vector.tensor_tensor(
                        out=low_e, in0=low_src[:, :].unsqueeze(2).to_broadcast([P, TILES, NT]),
                        in1=iota_b[:, :].unsqueeze(1).to_broadcast([P, TILES, NT]), op=ALU.is_equal))
                    then(nc.vector.tensor_tensor(out=picked, in0=by_tile[:, :, 0:NT], in1=low_e, op=ALU.mult))
                    then(nc.vector.tensor_reduce(out=root_src[:], in_=picked, axis=AX.X, op=ALU.add))
                    dve.wait_ge(early_copied, n + 1)
                    dve.wait_ge(attr_e_loaded, (n + 1) * 16)
                    nc.vector.tensor_tensor(out=attr_e, in0=attr_e, in1=feat_e[:, :, D:2 * D],
                                            op=ALU.add).then_inc(early_summed, 1)
                    dve.wait_ge(early_product, n + 1)
                    window_hots(hot_e, c)
                    then(nc.vector.tensor_tensor(out=wroot_e[:], in0=e_w[:, c], in1=root_src[:], op=ALU.mult))
                    weigh(hot_e, 1, e_w[:, c])
                    weigh(hot_e, 2, wroot_e[:, :]).then_inc(early_hots_ready, 1)

                with dve.Fori(0, EARLY) as i:
                    late_step(i, True)
                with dve.Fori(EARLY, LATE_STEPS) as i:
                    late_step(i, False)

            def per_node(t, tiles):
                return t[:, tiles].unsqueeze(2).to_broadcast([P, GROUP, D])

            for g in range(GROUPS):
                tiles, s = slice(g * GROUP, (g + 1) * GROUP), g % 2
                t0, t1 = h_tmp[:, 2 * s], h_tmp[:, 2 * s + 1]
                dve.wait_ge(out_product, g + 1)
                nc.vector.tensor_tensor(out=t0, in0=pair_ps[s][:, :, 0:D], in1=per_node(inv_root, tiles), op=ALU.mult)
                nc.vector.tensor_tensor(out=h[:, tiles], in0=sum_ps[s], in1=h_node[:, tiles], op=ALU.add)
                nc.vector.tensor_tensor(out=t1, in0=pair_ps[s][:, :, D:2 * D], in1=per_node(inv_count, tiles),
                                        op=ALU.mult).then_inc(out_taken, 1)
                dve.wait_ge(out_taken, g + 1)
                link(nc.vector.tensor_tensor(out=t0, in0=t0, in1=t1, op=ALU.add))
                link(nc.vector.tensor_tensor(out=h[:, tiles], in0=h[:, tiles], in1=t0, op=ALU.add))
                link(nc.vector.tensor_reduce(out=mean[:, tiles], in_=h[:, tiles], axis=AX.X, op=ALU.add))
                link(nc.vector.tensor_scalar(mean[:, tiles], mean[:, tiles], 1.0 / D, None, ALU.mult))
                nc.vector.tensor_tensor(out=h[:, tiles], in0=h[:, tiles], in1=per_node(mean, tiles), op=ALU.subtract).then_inc(centred, 1)
                dve.wait_ge(squared, g + 1)
                nc.vector.tensor_reduce(out=var[:, tiles], in_=squares[:, s], axis=AX.X, op=ALU.add).then_inc(var_ready, 1)
                dve.wait_ge(root_ready, g + 1)
                link(nc.vector.reciprocal(var[:, tiles], deg_root[:, tiles]))
                nc.vector.tensor_tensor(out=h[:, tiles], in0=h[:, tiles], in1=per_node(var, tiles), op=ALU.mult).then_inc(out_ready, 1)

        @block.tensor
        def _(pe):
            pe.sem_inc(chunk_product, UNROLL)
            pe.sem_inc(roots_product, 1)
            pe.sem_inc(early_product, 1)
            pe.wait_ge(consts, 4)
            pe.wait_ge(unfit_ready, 1)
            nc.tensor.matmul(misc_ps[:, 0:1], ones[:], unfit_any[:], start=True, stop=True).then_inc(unfit_counted, 1)
            pe.wait_ge(base_ready, 1)
            for g, n in groups:
                last = nc.tensor.transpose(misc_ps[0:1, P + g * P:P + g * P + n], base[0:n, g:g + 1], ident[0:n, 0:n])
            last.then_inc(base_flipped, 1)
            q = 0
            for k, rows in enumerate((row_dst, row_w, row_src)):
                if k == 1:
                    pe.wait_ge(w_loaded, ROWS_LOADED)
                for g, n in groups:
                    if k == 2:
                        pe.wait_ge(rows_ready, g + 1)
                    v = rows[:, g].rearrange("c (p j) -> c j p", j=TILES)
                    for half in range(TILES // 4):
                        q += 1
                        if 2 < q <= DST_FLIPS + 2:
                            pe.wait_ge(dst_flip_used, q - 2)
                        elif q > DST_FLIPS + 2:
                            pe.wait_ge(flip_used, q - 2 - DST_FLIPS)
                        for j in range(4):
                            last = nc.tensor.transpose(flip_ps[(q - 1) % 2][:, j * P:j * P + n],
                                                       v[0:n, 4 * half + j], ident[0:n, 0:n])
                        last.then_inc(flipped, 1)
            pe.wait_ge(base_stored, 1)
            n_pass = pe.value_load(passes[0:1, 0:1], min_val=1, max_val=WINDOWS)
            pe.sem_inc(deg_product, DEG_SLOTS)
            with pe.Fori(0, n_pass) as v:
                def sum_degrees(i, half):
                    for s in range(2):
                        slot, step = 2 * half + s, v * 2 * STEPS + i * 2 + s
                        pe.wait_ge(hot_b_ready, step + 1)
                        pe.wait_ge(w_staged, step + 1)
                        pe.wait_ge(deg_added, (step + 1) * DEG_CHUNKS)
                        for k in range(DEG_CHUNKS):
                            for j in range(TILES):
                                last = nc.tensor.matmul(deg_ps[slot][32 * k:32 * k + 4, 0:WINDOW], w_stage[:, slot, k, j],
                                                        hot_b[:, slot, :, k * TILES + j], start=(j == 0), stop=(j == TILES - 1))
                        last.then_inc(deg_product, 1)

                with pe.Fori(0, STEPS // 2) as i2:
                    sum_degrees(i2 * 2, 0)
                    sum_degrees(i2 * 2 + 1, 1)
                sum_degrees(STEPS - 1, 0)
            pe.wait_ge(deg_summed, 1)
            pe.wait_ge(x_loaded, X_LOADED)
            pe.wait_ge(flip_used, FLIPS - DST_FLIPS)
            for g in range(GROUPS + 1):
                if g < GROUPS:
                    if g >= 2:
                        pe.wait_ge(x_flip_used, g - 1)
                    for n in range(GROUP):
                        last = nc.tensor.transpose(x_ps[g % 2][:, n * P:(n + 1) * P], table_sb[:, g * GROUP + n, 0:D], ident[:])
                    last.then_inc(x_flipped, 1)
                if g == 1:
                    pe.wait_ge(weights_mixed, 1)
                if g > 0:
                    pe.wait_ge(x_flip_used, g)
                    if g > 2:
                        pe.wait_ge(node_taken, g - 2)
                    for n in range(GROUP):
                        last = nc.tensor.matmul(node_ps[(g - 1) % 2][:, n * D:(n + 1) * D],
                                                xT[:, (g - 1) % 2, n * P:(n + 1) * P], W_node[:, :], start=True, stop=True)
                    last.then_inc(node_product, 1)
            with pe.Fori(0, n_pass) as v:
                def segment_sums(to, features, hots):
                    for j in range(TILES):
                        last = nc.tensor.matmul(to[:, 0:3 * WINDOW], features[:, j, 0:2 * D],
                                                hots[:, j].rearrange("p k n -> p (k n)"),
                                                start=(j == 0), stop=(j == TILES - 1))
                    return last

                def late_step(i, early):
                    if early:
                        pe.wait_ge(high_ready, v * EARLY + i + 1)
                        for j in range(TILES):
                            last = nc.tensor.matmul(root_ps[:, j * (NT + 1):(j + 1) * (NT + 1)],
                                                    high_e[:, j:CHUNK:TILES], root_part[:, :], start=True, stop=True)
                        last.then_inc(roots_product, 1)
                    for u in range(UNROLL):
                        it = v * LATE + i * UNROLL + u
                        pe.wait_ge(relu_ready, it + 1 + UNROLL)
                        pe.wait_ge(hots_ready, it + 1)
                        pe.wait_ge(added, (it + 1) * 3)
                        segment_sums(acc_ps[u % 2], feat[:, u], hot[:, u]).then_inc(chunk_product, 1)
                        if early and u == 1:
                            pe.wait_ge(early_relu_ready, v * EARLY + i + 2)
                            pe.wait_ge(early_hots_ready, v * EARLY + i + 1)
                            pe.wait_ge(early_added, (v * EARLY + i + 1) * 3)
                            segment_sums(acc_e, feat_e, hot_e).then_inc(early_product, 1)

                with pe.Fori(0, EARLY) as i:
                    late_step(i, True)
                with pe.Fori(EARLY, LATE_STEPS) as i:
                    late_step(i, False)
            pe.wait_ge(early_added, (n_pass * EARLY + 1) * 3)
            pe.wait_ge(added, (n_pass * LATE + 2) * 3)
            pe.wait_ge(node_taken, GROUPS)
            for g in range(GROUPS):
                if g >= 2:
                    pe.wait_ge(out_taken, g - 1)
                for k, to, W in ((0, sum_ps[g % 2], W_sum[:, :]), (1, pair_ps[g % 2], W_pair[:, :, :].rearrange("p a d -> p (a d)"))):
                    for n in range(GROUP):
                        t = g * GROUP + n
                        last = nc.tensor.matmul(to[:, n], sums[:, k, t:t + (P - 1) * NT + 1:NT], W, start=True, stop=True)
                last.then_inc(out_product, 1)


INPUTS = ("x", "src", "dst", "edge_attr_64", "edge_weight", "L0_gnn_weights", "L0_gnn_Wgcn", "L0_gnn_bgcn",
          "L0_gnn_Wsage_s", "L0_gnn_Wsage_n", "L0_gnn_bsage", "L0_gnn_gin_eps", "L0_gnn_Wgin", "L0_gnn_bgin",
          "L0_gnn_Wgc1", "L0_gnn_Wgc2", "L0_gnn_bgc", "L0_gnn_Wedge", "L0_gnn_bedge")


def kernel(**inputs):
    import concourse.bacc as bacc
    from concourse.bass_utils import run_bass_kernel_spmd

    nc = bacc.Bacc("TRN2", target_bir_lowering=False, num_devices=1)
    arrays, args = {}, []
    for name in INPUTS:
        a = np.ascontiguousarray(inputs[name])
        if a.ndim == 0 or name.endswith("gin_eps"):
            a = a.reshape(1, 1)
        arrays[f"in_{name}"] = a
        args.append(nc.dram_tensor(f"in_{name}", a.shape, mybir.dt.from_np(a.dtype), kind="ExternalInput").ap())
    out = nc.dram_tensor("out", (N, D), F32, kind="ExternalOutput").ap()
    build(nc, *args, out)
    return run_bass_kernel_spmd(nc, [arrays], core_ids=[0]).results[0]["out"]
```
